# Optimizing a Trainium2 kernel written in Bass

```python
import numpy as np
import jax
import jax.numpy as jnp

def _softmax(x, axis=-1):
    return jax.nn.softmax(x, axis=axis)

def _gelu(x):
    return jax.nn.gelu(x, approximate=True)

def _silu(x):
    return jax.nn.silu(x)

def _sigmoid(x):
    return jax.nn.sigmoid(x)

def _layernorm(x, axis=-1, eps=1e-05):
    m = jnp.mean(x, axis=axis, keepdims=True)
    v = jnp.var(x, axis=axis, keepdims=True)
    return (x - m) / jnp.sqrt(v + eps)

def _scatter_add(tgt, idx, src, axis=0):
    return tgt.at[idx].add(src)

def _segment_sum(src, seg, n):
    return jax.ops.segment_sum(src, seg, n)
kernel_name = 'mk_pixart_seq_d2_seqx_r8_1662f1'

def setup_inputs(seed: int=0):
    np.random.seed(seed)
    _w = jnp.asarray

    def _rec_inputs():
        import jax
        import jax.numpy as jnp
        _rk = jax.random.key(seed)
        x = 7.22e-05 + 1 * jax.random.normal(jax.random.fold_in(_rk, 1), (4, 256, 128), jnp.float32)
        _lenS = 256 - jax.random.randint(jax.random.fold_in(_rk, 7), (4,), 0, max(1, 256 // 4) + 1, jnp.int32)
        _lenS2 = 512 - jax.random.randint(jax.random.fold_in(_rk, 8), (4,), 0, max(1, 512 // 4) + 1, jnp.int32)
        cond_1024 = 0.000887014 + 1.03683 * jax.random.normal(jax.random.fold_in(_rk, 11), (4, 128), jnp.float32)
        _ctx_1024P = jax.random.normal(jax.random.fold_in(_rk, 12), (4, 16, 128), jnp.float32)
        _ctx_1024c = jax.random.dirichlet(jax.random.fold_in(_rk, 512), 0.3 * jnp.ones((16,), jnp.float32), (4, 512))
        _ctx_1024t = jnp.einsum('bsk,bkd->bsd', _ctx_1024c, _ctx_1024P)
        _ctx_1024t = _ctx_1024t * jax.lax.rsqrt(jnp.mean(jnp.square(_ctx_1024t)) + 1e-12) * 0.953939
        ctx_1024 = 0.00086875 + 0.999764 * (_ctx_1024t + 0.3 * jax.random.normal(jax.random.fold_in(_rk, 612), (4, 512, 128), jnp.float32))
        return (x, cond_1024, ctx_1024)
    x, cond_1024, ctx_1024 = _rec_inputs()

    def _L0_xcond_setup():
        import jax, jax.numpy as jnp
        import numpy as np
        C = 128
        H = 16
        D = C // H
        WIN = 64
        SHIFT = 32
        TOPK = 16
        HID = 512
        EPS = 1e-06

        def _ln(x):
            x32 = x.astype(jnp.float32)
            m = x32.mean(-1, keepdims=True)
            v = jnp.mean((x32 - m) ** 2, axis=-1, keepdims=True)
            return ((x32 - m) * jax.lax.rsqrt(v + EPS)).astype(x.dtype)

        def _self_attn(h, w_qkv, b_qkv, w_so, b_so):
            B, L, _ = h.shape
            qkv = h @ w_qkv + b_qkv
            qkv = jnp.roll(qkv, -SHIFT, axis=1)
            nw = L // WIN
            qkv = qkv.reshape(B, nw, WIN, 3, H, D)
            q, k, v = (qkv[:, :, :, 0], qkv[:, :, :, 1], qkv[:, :, :, 2])
            scores = jnp.einsum('bnqhd,bnkhd->bnhqk', q, k) / jnp.sqrt(jnp.float32(D)).astype(h.dtype)
            attn = jax.nn.softmax(scores, axis=-1)
            o = jnp.einsum('bnhqk,bnkhd->bnqhd', attn, v).reshape(B, L, C)
            o = jnp.roll(o, SHIFT, axis=1)
            return o @ w_so + b_so

        def _topk_cross_attn(h, ctx, w_q, b_q, w_kv, b_kv, w_co, b_co):
            B, L, _ = h.shape
            Lc = ctx.shape[1]
            q = (h @ w_q + b_q).reshape(B, L, H, D)
            kv = (ctx @ w_kv + b_kv).reshape(B, Lc, 2, H, D)
            k, v = (kv[:, :, 0], kv[:, :, 1])
            scores = jnp.einsum('bqhd,bkhd->bhqk', q, k) / jnp.sqrt(jnp.float32(D)).astype(h.dtype)
            top_s, top_i = jax.lax.top_k(scores, TOPK)
            attn = jax.nn.softmax(top_s, axis=-1)
            v_bh = jnp.transpose(v, (0, 2, 1, 3))
            vg = jnp.take_along_axis(v_bh[:, :, None, :, :], top_i[..., None], axis=3)
            o = jnp.einsum('bhqk,bhqkd->bqhd', attn, vg).reshape(B, L, C)
            return o @ w_co + b_co

        def _swiglu(h, w_m1, b_m1, w_m2, b_m2):
            u = h @ w_m1 + b_m1
            a, b = (u[..., :HID], u[..., HID:])
            return jax.nn.silu(a) * b @ w_m2 + b_m2
        key = jax.random.key(seed)
        ks = jax.random.split(key, 24)
        s = 0.02
        inp = {'x': jax.random.normal(ks[0], (2, 512, C), jnp.float32), 'mod': jax.random.normal(ks[1], (2, C), jnp.float32), 'context': jax.random.normal(ks[2], (2, 128, C), jnp.float32), 'w_ada': jax.random.normal(ks[3], (C, 9 * C), jnp.float32) * s, 'b_ada': jnp.zeros((9 * C,), jnp.float32), 'w_qkv': jax.random.normal(ks[4], (C, 3 * C), jnp.float32) * s, 'b_qkv': jnp.zeros((3 * C,), jnp.float32), 'w_so': jax.random.normal(ks[5], (C, C), jnp.float32) * s, 'b_so': jnp.zeros((C,), jnp.float32), 'w_q': jax.random.normal(ks[6], (C, C), jnp.float32) * s, 'b_q': jnp.zeros((C,), jnp.float32), 'w_kv': jax.random.normal(ks[7], (C, 2 * C), jnp.float32) * s, 'b_kv': jnp.zeros((2 * C,), jnp.float32), 'w_co': jax.random.normal(ks[8], (C, C), jnp.float32) * s, 'b_co': jnp.zeros((C,), jnp.float32), 'w_m1': jax.random.normal(ks[9], (C, 2 * HID), jnp.float32) * s, 'b_m1': jnp.zeros((2 * HID,), jnp.float32), 'w_m2': jax.random.normal(ks[10], (HID, C), jnp.float32) * s, 'b_m2': jnp.zeros((C,), jnp.float32)}
        return inp
    _L0_xcond_all = _L0_xcond_setup()
    _L0_xcond_in = {k: v for k, v in _L0_xcond_all.items() if k in ('w_ada', 'b_ada', 'w_qkv', 'b_qkv', 'w_so', 'b_so', 'w_q', 'b_q', 'w_kv', 'b_kv', 'w_co', 'b_co', 'w_m1', 'b_m1', 'w_m2', 'b_m2')}
    del _L0_xcond_all

    def _L1_xcond_setup():
        import jax, jax.numpy as jnp
        import numpy as np
        EPS = 1e-05

        def _ada_ln(x, c, W_ss, b_ss):
            mu = jnp.mean(x, axis=-1, keepdims=True)
            var = jnp.mean((x - mu) ** 2, axis=-1, keepdims=True)
            h = (x - mu) / jnp.sqrt(var + EPS)
            ss = jax.nn.silu(c) @ W_ss + b_ss
            scale, bias = jnp.split(ss, 2, axis=-1)
            return (1.0 + scale)[:, None, :] * h + bias[:, None, :]
        key = jax.random.key(seed)
        ks = jax.random.split(key, 12)
        B, Lq, Lkv, H = (8, 256, 64, 128)
        s = 0.02
        return {'x_q': jax.random.normal(ks[0], (B, Lq, H), jnp.float32), 'x_kv': jax.random.normal(ks[1], (B, Lkv, H), jnp.float32), 't_vec': jax.random.normal(ks[2], (B, H), jnp.float32), 'Wq': jax.random.normal(ks[3], (H, H), jnp.float32) * s, 'bq': jnp.zeros((H,), jnp.float32), 'Wkv': jax.random.normal(ks[4], (H, 2 * H), jnp.float32) * s, 'bkv': jnp.zeros((2 * H,), jnp.float32), 'Wp': jax.random.normal(ks[5], (H, H), jnp.float32) * s, 'bp': jnp.zeros((H,), jnp.float32), 'Wss_q': jax.random.normal(ks[6], (H, 2 * H), jnp.float32) * s, 'bss_q': jnp.zeros((2 * H,), jnp.float32), 'Wss_kv': jax.random.normal(ks[7], (H, 2 * H), jnp.float32) * s, 'bss_kv': jnp.zeros((2 * H,), jnp.float32)}
    _L1_xcond_all = _L1_xcond_setup()
    _L1_xcond_in = {k: v for k, v in _L1_xcond_all.items() if k in ('Wq', 'bq', 'Wkv', 'bkv', 'Wp', 'bp', 'Wss_q', 'bss_q', 'Wss_kv', 'bss_kv')}
    del _L1_xcond_all
    return {'x': x, 'cond_1024': cond_1024, 'ctx_1024': ctx_1024, 'L0_xcond_w_ada': _L0_xcond_in['w_ada'], 'L0_xcond_b_ada': _L0_xcond_in['b_ada'], 'L0_xcond_w_qkv': _L0_xcond_in['w_qkv'], 'L0_xcond_b_qkv': _L0_xcond_in['b_qkv'], 'L0_xcond_w_so': _L0_xcond_in['w_so'], 'L0_xcond_b_so': _L0_xcond_in['b_so'], 'L0_xcond_w_q': _L0_xcond_in['w_q'], 'L0_xcond_b_q': _L0_xcond_in['b_q'], 'L0_xcond_w_kv': _L0_xcond_in['w_kv'], 'L0_xcond_b_kv': _L0_xcond_in['b_kv'], 'L0_xcond_w_co': _L0_xcond_in['w_co'], 'L0_xcond_b_co': _L0_xcond_in['b_co'], 'L0_xcond_w_m1': _L0_xcond_in['w_m1'], 'L0_xcond_b_m1': _L0_xcond_in['b_m1'], 'L0_xcond_w_m2': _L0_xcond_in['w_m2'], 'L0_xcond_b_m2': _L0_xcond_in['b_m2'], 'L1_xcond_Wq': _L1_xcond_in['Wq'], 'L1_xcond_bq': _L1_xcond_in['bq'], 'L1_xcond_Wkv': _L1_xcond_in['Wkv'], 'L1_xcond_bkv': _L1_xcond_in['bkv'], 'L1_xcond_Wp': _L1_xcond_in['Wp'], 'L1_xcond_bp': _L1_xcond_in['bp'], 'L1_xcond_Wss_q': _L1_xcond_in['Wss_q'], 'L1_xcond_bss_q': _L1_xcond_in['bss_q'], 'L1_xcond_Wss_kv': _L1_xcond_in['Wss_kv'], 'L1_xcond_bss_kv': _L1_xcond_in['bss_kv']}

def reference(x, cond_1024, ctx_1024, L0_xcond_w_ada, L0_xcond_b_ada, L0_xcond_w_qkv, L0_xcond_b_qkv, L0_xcond_w_so, L0_xcond_b_so, L0_xcond_w_q, L0_xcond_b_q, L0_xcond_w_kv, L0_xcond_b_kv, L0_xcond_w_co, L0_xcond_b_co, L0_xcond_w_m1, L0_xcond_b_m1, L0_xcond_w_m2, L0_xcond_b_m2, L1_xcond_Wq, L1_xcond_bq, L1_xcond_Wkv, L1_xcond_bkv, L1_xcond_Wp, L1_xcond_bp, L1_xcond_Wss_q, L1_xcond_bss_q, L1_xcond_Wss_kv, L1_xcond_bss_kv):
    import jax
    import jax.numpy as jnp

    def _L0_xcond_ref(x, mod, context, w_ada, b_ada, w_qkv, b_qkv, w_so, b_so, w_q, b_q, w_kv, b_kv, w_co, b_co, w_m1, b_m1, w_m2, b_m2):
        import jax, jax.numpy as jnp
        import numpy as np
        C = 128
        H = 16
        D = C // H
        WIN = 64
        SHIFT = 32
        TOPK = 16
        HID = 512
        EPS = 1e-06

        def _ln(x):
            x32 = x.astype(jnp.float32)
            m = x32.mean(-1, keepdims=True)
            v = jnp.mean((x32 - m) ** 2, axis=-1, keepdims=True)
            return ((x32 - m) * jax.lax.rsqrt(v + EPS)).astype(x.dtype)

        def _self_attn(h, w_qkv, b_qkv, w_so, b_so):
            B, L, _ = h.shape
            qkv = h @ w_qkv + b_qkv
            qkv = jnp.roll(qkv, -SHIFT, axis=1)
            nw = L // WIN
            qkv = qkv.reshape(B, nw, WIN, 3, H, D)
            q, k, v = (qkv[:, :, :, 0], qkv[:, :, :, 1], qkv[:, :, :, 2])
            scores = jnp.einsum('bnqhd,bnkhd->bnhqk', q, k) / jnp.sqrt(jnp.float32(D)).astype(h.dtype)
            attn = jax.nn.softmax(scores, axis=-1)
            o = jnp.einsum('bnhqk,bnkhd->bnqhd', attn, v).reshape(B, L, C)
            o = jnp.roll(o, SHIFT, axis=1)
            return o @ w_so + b_so

        def _topk_cross_attn(h, ctx, w_q, b_q, w_kv, b_kv, w_co, b_co):
            B, L, _ = h.shape
            Lc = ctx.shape[1]
            q = (h @ w_q + b_q).reshape(B, L, H, D)
            kv = (ctx @ w_kv + b_kv).reshape(B, Lc, 2, H, D)
            k, v = (kv[:, :, 0], kv[:, :, 1])
            scores = jnp.einsum('bqhd,bkhd->bhqk', q, k) / jnp.sqrt(jnp.float32(D)).astype(h.dtype)
            top_s, top_i = jax.lax.top_k(scores, TOPK)
            attn = jax.nn.softmax(top_s, axis=-1)
            v_bh = jnp.transpose(v, (0, 2, 1, 3))
            vg = jnp.take_along_axis(v_bh[:, :, None, :, :], top_i[..., None], axis=3)
            o = jnp.einsum('bhqk,bhqkd->bqhd', attn, vg).reshape(B, L, C)
            return o @ w_co + b_co

        def _swiglu(h, w_m1, b_m1, w_m2, b_m2):
            u = h @ w_m1 + b_m1
            a, b = (u[..., :HID], u[..., HID:])
            return jax.nn.silu(a) * b @ w_m2 + b_m2
        m = jax.nn.silu(mod) @ w_ada + b_ada
        sh_msa, sc_msa, g_msa, sh_mca, sc_mca, g_mca, sh_mlp, sc_mlp, g_mlp = [m[:, i * C:(i + 1) * C][:, None, :] for i in range(9)]
        h = _ln(x) * (1 + sc_msa) + sh_msa
        h = _self_attn(h, w_qkv, b_qkv, w_so, b_so)
        x = x + h * g_msa
        h = _ln(x) * (1 + sc_mca) + sh_mca
        h = _topk_cross_attn(h, context, w_q, b_q, w_kv, b_kv, w_co, b_co)
        x = x + h * g_mca
        h = _ln(x) * (1 + sc_mlp) + sh_mlp
        h = _swiglu(h, w_m1, b_m1, w_m2, b_m2)
        x = x + h * g_mlp
        return x

    def _L1_xcond_ref(x_q, x_kv, t_vec, Wq, bq, Wkv, bkv, Wp, bp, Wss_q, bss_q, Wss_kv, bss_kv):
        import jax, jax.numpy as jnp
        import numpy as np
        EPS = 1e-05

        def _ada_ln(x, c, W_ss, b_ss):
            mu = jnp.mean(x, axis=-1, keepdims=True)
            var = jnp.mean((x - mu) ** 2, axis=-1, keepdims=True)
            h = (x - mu) / jnp.sqrt(var + EPS)
            ss = jax.nn.silu(c) @ W_ss + b_ss
            scale, bias = jnp.split(ss, 2, axis=-1)
            return (1.0 + scale)[:, None, :] * h + bias[:, None, :]
        B, Lq, H = x_q.shape
        Lkv = x_kv.shape[1]
        nh = 16
        dh = H // nh
        xq = _ada_ln(x_q, t_vec, Wss_q, bss_q)
        xkv = _ada_ln(x_kv, t_vec, Wss_kv, bss_kv)
        q = (xq @ Wq + bq).reshape(B, Lq, nh, dh)
        kv = (xkv @ Wkv + bkv).reshape(B, Lkv, 2, nh, dh)
        k = kv[:, :, 0]
        v = kv[:, :, 1]
        scores = jnp.einsum('bqhd,bkhd->bhqk', q, k) / jnp.sqrt(jnp.float32(dh))
        attn = jax.nn.softmax(scores, axis=-1)
        out = jnp.einsum('bhqk,bkhd->bqhd', attn, v).reshape(B, Lq, H)
        return x_q + (out @ Wp + bp)
    x = _L0_xcond_ref(x, cond_1024, ctx_1024, L0_xcond_w_ada, L0_xcond_b_ada, L0_xcond_w_qkv, L0_xcond_b_qkv, L0_xcond_w_so, L0_xcond_b_so, L0_xcond_w_q, L0_xcond_b_q, L0_xcond_w_kv, L0_xcond_b_kv, L0_xcond_w_co, L0_xcond_b_co, L0_xcond_w_m1, L0_xcond_b_m1, L0_xcond_w_m2, L0_xcond_b_m2)
    x = _L1_xcond_ref(x, ctx_1024, cond_1024, L1_xcond_Wq, L1_xcond_bq, L1_xcond_Wkv, L1_xcond_bkv, L1_xcond_Wp, L1_xcond_bp, L1_xcond_Wss_q, L1_xcond_bss_q, L1_xcond_Wss_kv, L1_xcond_bss_kv)
    return x

_drawn_inputs = setup_inputs


def setup_inputs(seed=0):
    import zlib

    import numpy as np

    out = dict(_drawn_inputs(seed))
    spreads = {'L0_xcond_b_ada': (0.0, 0.417),
     'L0_xcond_b_qkv': (0.0, 0.8),
     'L0_xcond_b_so': (0.0, 0.451),
     'L0_xcond_b_q': (0.0, 0.8),
     'L0_xcond_b_kv': (0.0, 0.8),
     'L0_xcond_b_co': (0.0, 0.465),
     'L0_xcond_b_m1': (0.0, 0.8),
     'L0_xcond_b_m2': (0.0, 0.431),
     'L1_xcond_bq': (0.0, 2.0),
     'L1_xcond_bkv': (0.0, 2.0),
     'L1_xcond_bp': (0.0, 0.516),
     'L1_xcond_bss_q': (0.0, 2.0),
     'L1_xcond_bss_kv': (0.0, 2.0)}
    factors = {'L0_xcond_w_qkv': 8.0,
     'L0_xcond_w_so': 8.0,
     'L0_xcond_w_q': 8.0,
     'L0_xcond_w_kv': 8.0,
     'L0_xcond_w_co': 6.732,
     'L0_xcond_w_m1': 8.0,
     'L0_xcond_w_m2': 8.0,
     'L1_xcond_Wq': 64.0,
     'L1_xcond_Wss_q': 64.0,
     'L1_xcond_Wss_kv': 41.591,
     'L1_xcond_Wkv': 4.751,
     'L1_xcond_Wp': 3.106}
    for name, (base, spread) in spreads.items():
        noise = np.random.default_rng([zlib.crc32(name.encode()), seed]).standard_normal(out[name].shape)
        drawn = base * np.exp(spread * noise) if base else spread * noise
        out[name] = jnp.asarray(drawn.astype(out[name].dtype))
    for name, factor in factors.items():
        out[name] = (out[name] * factor).astype(out[name].dtype)
    return out
```

```python
from contextlib import ExitStack

import concourse.bass as bass
from concourse import mybir

F32 = mybir.dt.float32
BF16 = mybir.dt.bfloat16
ALU = mybir.AluOpType
ACT = mybir.ActivationFunctionType
AX_X = mybir.AxisListType.X

P = 128
B, L, LC, C = 4, 256, 512, 128
H = 16
D = C // H
HID = 512
WIN, SHIFT = 64, 32
EPS0, EPS1 = 1e-6, 1e-5
SCALE = float(D) ** -0.5
TAKEN = -3.0e38
OFF_WINDOW = -1.0e30

NTOK = B * L
NCTX = B * LC
NT = NTOK // P
NCT = NCTX // P
CH = 512
NX = NTOK // CH
KC = LC // P
DV = D + 1

Q_PART = (0, 0, 0, 1, 1, 2)
K_PART = (0, 1, 2, 0, 1, 0)
KS = D * len(Q_PART)

VECTORS = (
    ("L0_xcond_b_ada", 9), ("L1_xcond_bss_q", 2), ("L1_xcond_bss_kv", 2), ("L0_xcond_b_qkv", 3),
    ("L0_xcond_b_so", 1), ("L0_xcond_b_q", 1), ("L0_xcond_b_kv", 2), ("L0_xcond_b_co", 1),
    ("L0_xcond_b_m1", 8), ("L0_xcond_b_m2", 1), ("L1_xcond_bq", 1), ("L1_xcond_bkv", 2),
    ("L1_xcond_bp", 1),
)
COL = {}
_at = 0
for _name, _rows in VECTORS:
    COL[_name] = _at
    _at += _rows
COND_AT = _at
NVEC = _at + B
NMOD = 13
SH_MSA, SC_MSA, G_MSA, SH_MCA, SC_MCA, G_MCA, SH_MLP, SC_MLP, G_MLP, SC_Q, SH_Q, SC_KV, SH_KV = range(NMOD)


def pixart_kernel(nc, a, out):
    with ExitStack() as ctx:
        def sb(name, shape, dt=F32):
            return ctx.enter_context(nc.sbuf_tensor(name, shape, dt))

        def sem(name):
            return ctx.enter_context(nc.semaphore(name))

        ident = sb("ident", [P, P])
        mean_w = sb("mean_w", [P, P])
        neg_scale = sb("neg_scale", [P, 1])
        winq = sb("winq", [2, NTOK], BF16)
        wink = sb("wink", [2, NTOK], BF16)
        vecs = sb("vecs", [NVEC, P])
        vecs_p = sb("vecs_p", [NVEC, P])
        w_qk = sb("w_qk", [P, 6, C])
        cols = sb("cols", [P, 2, NVEC])
        half_b1 = sb("half_b1", [P, 4])
        w_ada = sb("w_ada", [P, 9 * C])
        w_qkv = sb("w_qkv", [P, 3 * C])
        w_so = sb("w_so", [P, C])
        w_q = sb("w_q", [P, C])
        w_kv = sb("w_kv", [P, 2 * C])
        w_co = sb("w_co", [P, C])
        w_m1 = sb("w_m1", [P, 2 * HID])
        w_m2 = sb("w_m2", [P, HID // P, C])
        w1_q = sb("w1_q", [P, C])
        w1_kv = sb("w1_kv", [P, 2 * C])
        w1_p = sb("w1_p", [P, C])
        w_ss = sb("w_ss", [P, 4 * C])
        silu_c = sb("silu_c", [P, B])
        silu_e = sb("silu_e", [P, B])
        mods = sb("mods", [P, NMOD, B])
        tok = sb("tok", [P, NT, P])
        xT = sb("xT", [P, NTOK])
        ctxT = sb("ctxT", [P, NCTX])
        ctxhT = sb("ctxhT", [P, NCTX])
        ctx_tok = ctxhT[:].rearrange("p (t f) -> p t f", f=P)
        q_stack = sb("q_stack", [KS + 2, B * H * L], BF16)
        k_stack = sb("k_stack", [KS + 2, B * H * LC], BF16)
        v_self = sb("v_self", [P, NT, H, DV])
        v_ctx = sb("v_ctx", [P, B, H, KC, DV])
        o_raw = sb("o_raw", [P, B, H, 2, DV])
        rden = sb("rden", [P, B, H, 2])
        top = sb("top", [P, 4, 16])
        nmax = sb("nmax", [P, 4, 4])
        work = sb("work", [P, 13, CH])

        def e_buf(j):
            return work[:, j, :]

        def s2_buf(j):
            return work[:, 4 + j, :]

        def pT_buf(j):
            return work[:, 8 + j, :]

        s1_buf = work[:, 12, :]

        def xc_buf(c):
            return work[:, c % 2, :]

        def sq_buf(c):
            return work[:, 2 + c % 2, :]

        hT = work[:, 4:6, :].rearrange("p c n -> p (c n)")

        def full_buf(i):
            return work[:, 6 + i % 2, :]

        def rest_buf(i):
            return work[:, 8 + i % 2, :]

        parts_all = work[:, 10:13, :].bitcast(BF16).rearrange("p a n -> p (a n)").rearrange(
            "p (r s n) -> p r s n", r=2, s=3)

        def part_buf(i, s):
            return parts_all[:, i % 2, s, :]

        bank = [ctx.enter_context(nc.psum_tensor(f"bank{i}", [P, 512], F32)) for i in range(8)]
        O_BANK = 6

        ones_set = sem("ones_set")
        ident_set = sem("ident_set")
        win_set = sem("win_set")
        vec_in = sem("vec_in")
        x_in = sem("x_in")
        ctx_in = sem("ctx_in")
        ada_in = sem("ada_in")
        w_in = sem("w_in")
        win_in = sem("win_in")
        cols_T = sem("cols_T")
        cols_set = sem("cols_set")
        vecs_set = sem("vecs_set")
        w_qk_set = sem("w_qk_set")
        cond_step = sem("cond_step")
        silu_exp = sem("silu_exp")
        silu_set = sem("silu_set")
        mods_mm = sem("mods_mm")
        mods_set = sem("mods_set")
        x_T = sem("x_T")
        xT_set = sem("xT_set")
        ctx_T = sem("ctx_T")
        ctxT_set = sem("ctxT_set")
        out_T = sem("out_T")
        out_set = [sem(f"out_set{c}") for c in range(NX)]
        stored = sem("stored")

        def stage_sems(names, stage):
            return {n: sem(f"{n}_{stage}") for n in names}

        ln = stage_sems(("mean_mm", "centred", "squared", "var_mm", "log_var", "rstd", "normed", "modulated"), "norm")
        LN_AT = {"ctx": 0, "self": B, "cross": B + NX, "mlp": B + 2 * NX, "last": B + 3 * NX}
        MODULATED_AT = {"ctx": 0, "self": B, "cross": 2 * B, "mlp": 3 * B, "last": 4 * B}
        sp_ = stage_sems(("full_mm", "full", "part0", "rest", "part1", "part2", "stacked0", "stacked1", "v_mm", "v_set"), "split")
        UNIT_AT = {"self": 0, "cross": 2 * NX, "last": 3 * NX + B}
        V_AT = {"self": 0, "cross": NT, "last": NT + NCT}
        fin = stage_sems(("recip", "o_norm", "o_T", "oT_set", "y_mm", "y_set", "x_new"), "out")
        FIN_AT = {"self": 0, "cross": 1, "last": 2}
        lp = {
            "self": stage_sems(("scores", "topped", "scanned", "expd", "p_T", "pT_set", "pv", "o_set"), "self"),
            "cross": stage_sems(("scores", "topped", "nm", "scanned", "expd", "marked", "masked", "p_ready", "p_T",
                                 "pT_set", "pv", "o_set"), "cross"),
            "last": stage_sems(("scores", "topped", "nm", "expd", "p_T", "pT_set", "pT_odd", "pv", "o_set"), "last"),
        }
        chain = sem("chain")
        turn = sem("turn")
        mlp = stage_sems(("a_mm", "b_mm", "a_set", "tanh_set", "gated", "hidden", "y_part", "y_set", "x_new"), "mlp")

        x_before = {"self": (xT_set, 2), "cross": (fin["x_new"], NX), "mlp": (fin["x_new"], 2 * NX),
                    "last": (mlp["x_new"], NX)}
        LN_OF = {
            "self": (xT, hT, NX, EPS0, SC_MSA, SH_MSA, 2),
            "cross": (xT, hT, NX, EPS0, SC_MCA, SH_MCA, 2),
            "mlp": (xT, hT, NX, EPS0, SC_MLP, SH_MLP, 2),
            "last": (xT, hT, NX, EPS1, SC_Q, SH_Q, 2),
            "ctx": (ctxT, ctxhT, B, EPS1, SC_KV, SH_KV, 1),
        }

        def chunk(t, c):
            return t[:, c * CH:(c + 1) * CH]

        bqkv, bkv, b1kv = COL["L0_xcond_b_qkv"], COL["L0_xcond_b_kv"], COL["L1_xcond_bkv"]
        PROJ = {
            "self": ([(w_qk[:, 0, :], bqkv, hT, NX, "q"), (w_qk[:, 1, :], bqkv + 1, hT, NX, "k")],
                     w_qkv[:, 2 * C:3 * C], hT, NT),
            "cross": ([(w_qk[:, 3, :], bkv, ctxT, B, "k"), (w_qk[:, 2, :], COL["L0_xcond_b_q"], hT, NX, "q")],
                      w_kv[:, C:2 * C], ctxT, NCT),
            "last": ([(w_qk[:, 5, :], b1kv, ctxhT, B, "k"), (w_qk[:, 4, :], COL["L1_xcond_bq"], hT, NX, "q")],
                     w1_kv[:, C:2 * C], ctxhT, NCT),
        }
        OUT = {
            "self": (w_so[:], COL["L0_xcond_b_so"], bqkv + 2, G_MSA),
            "cross": (w_co[:], COL["L0_xcond_b_co"], bkv + 1, G_MCA),
            "last": (w1_p[:], COL["L1_xcond_bp"], b1kv + 1, None),
        }

        def units(stage):
            n = UNIT_AT[stage]
            for w, col, src, chunks, kind in PROJ[stage][0]:
                for c in range(chunks):
                    yield w, col, src, c, kind, n
                    n += 1

        stacked_after, _dmas = {}, [0, 0]
        for _stage in PROJ:
            for _, _, _, _, _kind, _n in units(_stage):
                _dmas[_n % 2] += len(Q_PART) * (2 if _kind == "q" or _stage == "self" else 1)
                stacked_after[_n] = 16 * _dmas[_n % 2]

        block = ctx.enter_context(nc.Block())

        @block.sync
        def _(sp):
            for name, rows in VECTORS:
                at = COL[name]
                sp.dma_start(vecs[at:at + rows, :], a[name].rearrange("(r n) -> r n", n=P)).then_inc(vec_in, 16)
            sp.dma_start(vecs[COND_AT:NVEC, :], a["cond_1024"]).then_inc(vec_in, 16)
            x = a["x"]
            tiles = tok[:].rearrange("p (b h) f -> p b h f", h=2)
            sp.dma_start(tiles[:, :, 0, :], x[:, SHIFT:SHIFT + P, :].rearrange("b p f -> p b f")).then_inc(x_in, 16)
            sp.dma_start(tiles[0:P - SHIFT, :, 1, :],
                         x[:, SHIFT + P:L, :].rearrange("b p f -> p b f")).then_inc(x_in, 16)
            sp.dma_start(tiles[P - SHIFT:P, :, 1, :],
                         x[:, 0:SHIFT, :].rearrange("b p f -> p b f")).then_inc(x_in, 16)
            sp.wait_ge(win_set, 3)
            for h in range(H):
                sp.dma_start(q_stack[KS:KS + 2, :].rearrange("r (b h n) -> r b h n", b=B, h=H)[:, :, h, :],
                             winq[:].rearrange("r (b n) -> r b n", b=B)).then_inc(win_in, 16)
                sp.dma_start(k_stack[KS:KS + 2, 0:B * H * L].rearrange("r (b h n) -> r b h n", b=B, h=H)[:, :, h, :],
                             wink[:].rearrange("r (b n) -> r b n", b=B)).then_inc(win_in, 16)

            def stack(stage):
                s = sp_
                for _, _, _, c, kind, n in units(stage):
                    if kind == "q" or stage == "self":
                        whole = q_stack if kind == "q" else k_stack
                        dst = whole[:, 0:B * H * L].rearrange("r (b h n) -> r b h n", b=B, h=H)[:, 2 * c:2 * c + 2]
                    else:
                        dst = k_stack[:, :].rearrange("r (b h n) -> r b h n", b=B, h=H)[:, c:c + 1]
                    bb = dst.shape[1]
                    for t, part in enumerate(Q_PART if kind == "q" else K_PART):
                        if t == 0 and stage != "self":
                            before = "self" if stage == "cross" else "cross"
                            sp.wait_ge(lp[before]["scores"], NT * 4 if before == "self" else P)
                        sp.wait_ge(s[f"part{part}"], n + 1)
                        src = part_buf(n, part)
                        for i in range(bb):
                            sp.dma_start(dst[D * t:D * t + D, i],
                                         src.rearrange("p (b n) -> p b n", b=bb)[:, i]).then_inc(
                                s[f"stacked{n % 2}"], 16)

            stack("self")
            stack("cross")
            stack("last")
            for t in range(NT):
                b, half = divmod(t, 2)
                if half == 0:
                    sp.wait_ge(out_set[t // 4], 1)
                    sp.dma_start(out[b, SHIFT:SHIFT + P, :], tok[:, t, :]).then_inc(stored, 16)
                else:
                    sp.dma_start(out[b, SHIFT + P:L, :], tok[0:P - SHIFT, t, :]).then_inc(stored, 16)
                    sp.dma_start(out[b, 0:SHIFT, :], tok[P - SHIFT:P, t, :]).then_inc(stored, 16)
            sp.wait_ge(stored, 16 * 3 * B)

        @block.gpsimd
        def _(pool):
            g = nc.gpsimd
            g.memset(ident[:], 0.0).then_inc(ident_set, 1)
            g.memset(neg_scale[:], -SCALE).then_inc(ones_set, 1)
            g.memset(mean_w[:], 1.0 / C).then_inc(ones_set, 1)
            pool.wait_ge(ident_set, 1)
            g.affine_select(out=ident[:], in_=ident[:], compare_op=ALU.not_equal, fill=1.0, base=0,
                            pattern=[[-1, P]], channel_multiplier=1).then_inc(ident_set, 1)
            g.memset(winq[:], 1.0).then_inc(win_set, 1)
            pool.wait_ge(win_set, 1)
            wq = winq[:].rearrange("r (t w n) -> r t w n", w=2, n=WIN)
            g.affine_select(out=wq, in_=wq, compare_op=ALU.is_equal, fill=0.0, base=0,
                            pattern=[[0, NT], [-1, 2], [0, WIN]], channel_multiplier=1).then_inc(win_set, 1)
            pool.wait_ge(win_set, 2)
            g.tensor_scalar(wink[:], winq[:], -OFF_WINDOW, OFF_WINDOW, ALU.mult, ALU.add).then_inc(win_set, 1)
            pool.dma_start(w_ada[:], a["L0_xcond_w_ada"]).then_inc(ada_in, 16)
            pool.dma_start(w_ss[:, 0:2 * C], a["L1_xcond_Wss_q"]).then_inc(ada_in, 16)
            pool.dma_start(w_ss[:, 2 * C:], a["L1_xcond_Wss_kv"]).then_inc(ada_in, 16)
            g.memset(v_self[:, :, :, D:DV], 1.0).then_inc(ones_set, 1)
            g.memset(v_ctx[:, :, :, :, D:DV], 1.0).then_inc(ones_set, 1)

            pool.wait_ge(w_in, 160)
            for i, w in enumerate((w_qkv[:, 0:C], w_qkv[:, C:2 * C], w_q[:], w_kv[:, 0:C], w1_q[:], w1_kv[:, 0:C])):
                g.tensor_copy(w_qk[:, i, :].rearrange("p (d h) -> p d h", h=H),
                              w.rearrange("p (h d) -> p d h", h=H)).then_inc(w_qk_set, 1)

            def split_rest(stage):
                s = sp_
                for *_, n in units(stage):
                    pool.wait_ge(s["part0"], n + 1)
                    g.tensor_tensor(rest_buf(n), full_buf(n), part_buf(n, 0), ALU.subtract).then_inc(s["rest"], 1)
                    pool.wait_ge(s["part1"], n + 1)
                    g.tensor_tensor(part_buf(n, 2), rest_buf(n), part_buf(n, 1), ALU.subtract).then_inc(s["part2"], 1)

            split_rest("self")
            split_rest("cross")

            s = lp["cross"]

            def slot(n, j, first, last):
                t = 4 * n + j
                if not (first and j == 0):
                    jj = (j - 1) % 4
                    pool.wait_ge(s["masked"], t)
                    g.tensor_tensor(e_buf(jj), e_buf(jj), s2_buf(jj), ALU.subtract).then_inc(s["p_ready"], 1)
                if not last:
                    pool.wait_ge(s["topped"], t + 1)
                    g.tensor_tensor(nmax[:, j, 0:1], top[:, j, 0:1], neg_scale[:], ALU.mult).then_inc(s["nm"], 1)

            N = P // 4
            for j in range(4):
                slot(0, j, True, False)
            with pool.Fori(1, N) as n:
                for j in range(4):
                    slot(n, j, False, False)
            slot(N, 0, False, True)

            split_rest("last")
            s = lp["last"]

            def negate(n, j):
                pool.wait_ge(s["topped"], 4 * n + j + 1)
                g.tensor_tensor(nmax[:, j, 0:1], top[:, j, 0:1], neg_scale[:], ALU.mult).then_inc(s["nm"], 1)

            with pool.Fori(0, N) as n:
                for j in range(4):
                    negate(n, j)

        @block.scalar
        def _(act):
            s_ = nc.scalar
            act.dma_start(ctx_tok, a["ctx_1024"].rearrange("b (c p) f -> p (b c) f", p=P)).then_inc(ctx_in, 16)
            for dst, name in ((w_qkv[:], "L0_xcond_w_qkv"), (w_so[:], "L0_xcond_w_so"), (w_q[:], "L0_xcond_w_q"),
                              (w_kv[:], "L0_xcond_w_kv"), (w_co[:], "L0_xcond_w_co"), (w_m1[:], "L0_xcond_w_m1"),
                              (w1_q[:], "L1_xcond_Wq"), (w1_kv[:], "L1_xcond_Wkv"), (w1_p[:], "L1_xcond_Wp")):
                act.dma_start(dst, a[name]).then_inc(w_in, 16)
            act.dma_start(w_m2[:], a["L0_xcond_w_m2"].rearrange("(k p) n -> p k n", p=P)).then_inc(w_in, 16)
            act.wait_ge(cols_set, 1)
            s_.activation(silu_e[:], cols[:, 0, COND_AT:NVEC], ACT.Exp, scale=-1.0).then_inc(silu_exp, 1)
            act.wait_ge(x_T, 1)
            s_.activation(chunk(xT, 0), bank[0][:], ACT.Copy).then_inc(xT_set, 1)
            for c in (0, 2):
                act.wait_ge(ctx_T, c + 1)
                s_.activation(chunk(ctxT, c), bank[2 + c][:], ACT.Copy).then_inc(ctxT_set, 1)

            def norm(stage):
                s = ln
                at = LN_AT[stage]
                src, dst, chunks, eps, sc, sh, per = LN_OF[stage]
                for c0 in range(0, chunks, 2):
                    for c in (c0, c0 + 1):
                        act.wait_ge(s["centred"], at + c + 1)
                        s_.activation(sq_buf(c), xc_buf(c), ACT.Square).then_inc(s["squared"], 1)
                    for c in (c0, c0 + 1):
                        act.wait_ge(s["var_mm"], at + c + 1)
                        s_.activation(sq_buf(c), bank[2 * (c % 2) + 1][:], ACT.Ln, bias=eps).then_inc(s["log_var"], 1)
                    for c in (c0, c0 + 1):
                        act.wait_ge(s["log_var"], at + c + 1)
                        s_.activation(sq_buf(c), sq_buf(c), ACT.Exp, scale=-0.5).then_inc(s["rstd"], 1)
                    for c in (c0, c0 + 1):
                        act.wait_ge(s["normed"], at + c + 1)
                        if stage == "ctx" and c == 0:
                            act.wait_ge(mods_set, 2)
                        for i in range(per):
                            b = c * per + i
                            n = CH // per
                            s_.activation(dst[:, b * n:(b + 1) * n], xc_buf(c)[:, i * n:(i + 1) * n], ACT.Identity,
                                          scale=mods[:, sc, b:b + 1], bias=mods[:, sh, b:b + 1]).then_inc(
                                s["modulated"], 1)

            def split_full(stage):
                s = sp_
                for _, col, _, _, _, n in units(stage):
                    act.wait_ge(s["full_mm"], n + 1)
                    if n >= 2:
                        act.wait_ge(s["rest"], n - 1)
                    s_.activation(full_buf(n), bank[n % 2][:], ACT.Identity,
                                  bias=cols[:, 1, col:col + 1]).then_inc(s["full"], 1)

            def finish(stage):
                s = fin
                w, bcol, vcol, g = OUT[stage]
                for c in range(NX):
                    act.wait_ge(s["o_T"], NX * FIN_AT[stage] + c + 1)
                    s_.activation(chunk(hT, c), bank[2 * c][:], ACT.Identity,
                                  bias=cols[:, 0, vcol:vcol + 1]).then_inc(s["oT_set"], 1)
                for c in range(NX):
                    act.wait_ge(s["y_mm"], NX * FIN_AT[stage] + c + 1)
                    s_.activation(xc_buf(c), bank[2 * c + 1][:], ACT.Identity,
                                  bias=cols[:, 0, bcol:bcol + 1]).then_inc(s["y_set"], 1)

            norm("ctx")
            norm("self")
            split_full("self")

            s = lp["self"]
            N = NT

            def out_self(n):
                act.wait_ge(s["pv"], 4 * n + 4)
                dst = o_raw[:].rearrange("p b h t e -> p (b h t e)")
                dst = dst[:, bass.ds((n // 2) * (H * 2 * DV), H * 2 * DV)].rearrange("p (h t e) -> p h t e", h=H, t=2)
                s_.activation(dst[:, :, bass.ds(n % 2, 1), :].rearrange("p h t e -> p (h t) e"),
                              bank[O_BANK][:, 0:H * DV].rearrange("p (h e) -> p h e", h=H),
                              ACT.Copy).then_inc(s["o_set"], 1)

            def slot_self(n, j, first, last):
                t = 4 * n + j
                if not last:
                    act.wait_ge(s["scanned"], t + 1)
                    s_.activation(e_buf(j), e_buf(j), ACT.Exp, scale=SCALE).then_inc(s["expd"], 1)
                if not (first and j == 0):
                    act.wait_ge(s["p_T"], t)
                    if not (first and j < 4 + 1):
                        act.wait_ge(s["pv"], t - 4)
                    jj = (j - 1) % 4
                    s_.activation(pT_buf(jj), bank[4 + jj % 2][:], ACT.Copy).then_inc(s["pT_set"], 1)
                if j == 2 and not first:
                    out_self(n - 1)

            for j in range(4):
                slot_self(0, j, True, False)
            with act.Fori(1, N) as n:
                for j in range(4):
                    slot_self(n, j, False, False)
            slot_self(N, 0, False, True)
            out_self(N - 1)
            finish("self")
            norm("cross")
            split_full("cross")

            s = lp["cross"]
            N = P // 4

            def out_ctx(s, n):
                act.wait_ge(s["pv"], 4 * n + 4)
                dst = o_raw[:].rearrange("p b h t e -> p (b h t e)")
                s_.activation(dst[:, bass.ds(n * (4 * DV), 4 * DV)], bank[O_BANK][:, 0:4 * DV],
                              ACT.Copy).then_inc(s["o_set"], 1)

            def slot_cross(n, j, first, last):
                t = 4 * n + j
                jj = (j - 1) % 4
                prev = not (first and j == 0)
                if prev:
                    act.wait_ge(s["marked"], t)
                    s_.activation(s2_buf(jj), s2_buf(jj), ACT.Exp, scale=SCALE,
                                  bias=nmax[:, jj, 0:1]).then_inc(s["masked"], 1)
                if not last:
                    act.wait_ge(s["nm"], t + 1)
                    act.wait_ge(s["scanned"], t + 1)
                    if not first:
                        act.wait_ge(s["p_T"], t - 3)
                    s_.activation(e_buf(j), bank[j][:], ACT.Exp, scale=SCALE,
                                  bias=nmax[:, j, 0:1]).then_inc(s["expd"], 1)
                if prev:
                    act.wait_ge(s["p_T"], t)
                    if not first:
                        if not (type(n) is int and n == 1 and j == 0):
                            act.wait_ge(s["pv"], t - 4)
                    s_.activation(pT_buf(jj), bank[4 + jj % 2][:], ACT.Copy).then_inc(s["pT_set"], 1)
                if j == 2 and not first:
                    out_ctx(s, n - 1)

            for n0 in (0, 1):
                for j in range(4):
                    slot_cross(n0, j, n0 == 0, False)
            with act.Fori(2, N) as n:
                for j in range(4):
                    slot_cross(n, j, False, False)
            slot_cross(N, 0, False, True)
            out_ctx(s, N - 1)
            finish("cross")

            norm("mlp")
            for u in range(2 * 4):
                c, k = divmod(u, 4)
                bcol = COL["L0_xcond_b_m1"] + k
                act.wait_ge(mlp["a_mm"], u + 1)
                if u >= 2:
                    act.wait_ge(mlp["hidden"], u - 1)
                s_.activation(full_buf(u), bank[2 * (u % 2)][:], ACT.Identity,
                              bias=cols[:, 0, bcol:bcol + 1]).then_inc(mlp["a_set"], 1)
                s_.activation(rest_buf(u), bank[2 * (u % 2)][:], ACT.Tanh, scale=0.5,
                              bias=half_b1[:, k:k + 1]).then_inc(mlp["tanh_set"], 1)
            for c in range(NX):
                act.wait_ge(mlp["y_part"], 4 * (c + 1))
                bcol = COL["L0_xcond_b_m2"]
                s_.activation(xc_buf(c), bank[4 + c][:], ACT.Identity, scale=0.5,
                              bias=cols[:, 0, bcol:bcol + 1]).then_inc(mlp["y_set"], 1)

            norm("last")
            split_full("last")
            s = lp["last"]

            def slot_last(n, j, first, last):
                t = 4 * n + j
                jj = (j - 1) % 4
                if not last:
                    act.wait_ge(s["nm"], t + 1)
                    if not first:
                        act.wait_ge(s["p_T"], t - 3)
                    s_.activation(e_buf(j), bank[j][:], ACT.Exp, scale=SCALE,
                                  bias=nmax[:, j, 0:1]).then_inc(s["expd"], 1)
                if jj % 2 == 1 and not (first and j == 0):
                    act.wait_ge(s["p_T"], t)
                    if not (first or (type(n) is int and n == 1 and j == 0)):
                        act.wait_ge(s["pv"], t - 4)
                    s_.activation(pT_buf(jj), bank[4 + jj % 2][:], ACT.Copy).then_inc(s["pT_set"], 1)
                if j == 2 and not first:
                    out_ctx(s, n - 1)

            for n0 in (0, 1):
                for j in range(4):
                    slot_last(n0, j, n0 == 0, False)
            with act.Fori(2, N) as n:
                for j in range(4):
                    slot_last(n, j, False, False)
            slot_last(N, 0, False, True)
            out_ctx(s, N - 1)
            finish("last")
            act.wait_ge(out_T, 1)
            s_.activation(tok[:, 0:4, :].rearrange("p t f -> p (t f)"), bank[0][:], ACT.Copy).then_inc(out_set[0], 1)

        @block.vector
        def _(dve):
            v = nc.vector
            dve.wait_ge(vec_in, 16 * (len(VECTORS) + 1))
            v.tensor_copy(vecs_p[:].rearrange("r (d h) -> r d h", h=H),
                          vecs[:].rearrange("r (h d) -> r d h", h=H)).then_inc(vecs_set, 1)
            dve.wait_ge(cols_T, 1)
            v.tensor_copy(cols[:].rearrange("p a n -> p (a n)"), bank[7][:, 0:2 * NVEC]).then_inc(cols_set, 1)
            dve.wait_ge(cols_set, 1)
            v.tensor_scalar(half_b1[:], cols[:, 0, COL["L0_xcond_b_m1"]:COL["L0_xcond_b_m1"] + 4], 0.5, None,
                            ALU.mult).then_inc(cols_set, 1)
            dve.wait_ge(silu_exp, 1)
            v.tensor_scalar(silu_e[:], silu_e[:], 1.0, None, ALU.add).then_inc(cond_step, 1)
            dve.wait_ge(cond_step, 1)
            v.reciprocal(silu_e[:], silu_e[:]).then_inc(cond_step, 1)
            dve.wait_ge(cond_step, 2)
            v.tensor_tensor(silu_c[:], cols[:, 0, COND_AT:NVEC], silu_e[:], ALU.mult).then_inc(silu_set, 1)
            dve.wait_ge(mods_mm, 1)
            v.tensor_tensor(mods[:], bank[6][:, 0:NMOD * B].rearrange("p (m b) -> p m b", b=B),
                            cols[:, 0, 0:NMOD].unsqueeze(2).broadcast_to([P, NMOD, B]), ALU.add).then_inc(mods_set, 1)
            dve.wait_ge(mods_set, 1)
            scales = mods[:, 1:13, :].rearrange("p (m r) b -> p m r b", r=3)[:, 0:3, 0, :]
            v.tensor_scalar(scales, scales, 1.0, None, ALU.add).then_inc(cond_step, 1)
            scales = mods[:, 9:13, :].rearrange("p (m r) b -> p m r b", r=2)[:, :, 0, :]
            v.tensor_scalar(scales, scales, 1.0, None, ALU.add).then_inc(cond_step, 1)
            dve.wait_ge(cond_step, 4)
            dve.sem_inc(mods_set, 1)
            dve.wait_ge(x_T, 2)
            v.tensor_copy(chunk(xT, 1), bank[1][:]).then_inc(xT_set, 1)
            for c in (1, 3):
                dve.wait_ge(ctx_T, c + 1)
                v.tensor_copy(chunk(ctxT, c), bank[2 + c][:]).then_inc(ctxT_set, 1)

            def norm(stage):
                s = ln
                at = LN_AT[stage]
                src, dst, chunks, eps, sc, sh, per = LN_OF[stage]
                for c0 in range(0, chunks, 2):
                    for c in (c0, c0 + 1):
                        dve.wait_ge(s["mean_mm"], at + c + 1)
                        if c >= 2:
                            dve.wait_ge(s["modulated"], MODULATED_AT[stage] + per * (c - 1))
                        elif stage != "ctx":
                            dve.wait_ge(s["modulated"], MODULATED_AT[stage])
                        v.tensor_tensor(xc_buf(c), chunk(src, c), bank[2 * (c % 2)][:],
                                        ALU.subtract).then_inc(s["centred"], 1)
                    for c in (c0, c0 + 1):
                        dve.wait_ge(s["rstd"], at + c + 1)
                        v.tensor_tensor(xc_buf(c), xc_buf(c), sq_buf(c), ALU.mult).then_inc(s["normed"], 1)

            def split_parts(stage):
                s = sp_
                for _, _, _, _, kind, n in units(stage):
                    dve.wait_ge(s["full"], n + 1)
                    if n >= 2:
                        dve.wait_ge(s[f"stacked{n % 2}"], stacked_after[n - 2])
                    v.tensor_copy(part_buf(n, 0), full_buf(n)).then_inc(s["part0"], 1)
                    dve.wait_ge(s["rest"], n + 1)
                    v.tensor_copy(part_buf(n, 1), rest_buf(n)).then_inc(s["part1"], 1)

            def values(stage):
                s = sp_
                tiles = PROJ[stage][3]
                for g in range(tiles // 4):
                    dve.wait_ge(s["v_mm"], V_AT[stage] // 4 + g + 1)
                    if g == 0:
                        dve.wait_ge(ones_set, 4)
                    src = bank[2 + g % 2][:].rearrange("p (t h d) -> p t h d", t=4, h=H)
                    for i in range(4):
                        dst = v_self[:, 4 * g + i, :, 0:D] if stage == "self" else v_ctx[:, g, :, i, 0:D]
                        v.tensor_copy(dst, src[:, i]).then_inc(s["v_set"], 1)

            def finish(stage):
                s = fin
                w, bcol, vcol, g = OUT[stage]
                n_out = NT if stage == "self" else P // 4
                dve.wait_ge(lp[stage]["o_set"], n_out)
                v.reciprocal(rden[:], o_raw[:, :, :, :, D:DV].rearrange("p b h t e -> p b h (t e)")).then_inc(s["recip"], 1)
                dve.wait_ge(s["recip"], FIN_AT[stage] + 1)
                for b in range(B):
                    for t in range(2):
                        v.tensor_tensor(tok[:, 2 * b + t, :].rearrange("p (h d) -> p h d", h=H),
                                        o_raw[:, b, :, t, 0:D],
                                        rden[:, b, :, t:t + 1].broadcast_to([P, H, D]),
                                        ALU.mult).then_inc(s["o_norm"], 1)
                for c in range(NX):
                    dve.wait_ge(s["y_set"], NX * FIN_AT[stage] + c + 1)
                    if g is None:
                        v.tensor_tensor(chunk(xT, c), chunk(xT, c), xc_buf(c), ALU.add).then_inc(s["x_new"], 1)
                    else:
                        for i in range(2):
                            b = 2 * c + i
                            xb = xT[:, b * L:(b + 1) * L]
                            last = v.scalar_tensor_tensor(xb, xc_buf(c)[:, i * L:(i + 1) * L], mods[:, g, b:b + 1], xb,
                                                          ALU.mult, ALU.add)
                        last.then_inc(s["x_new"], 1)

            norm("ctx")
            norm("self")
            split_parts("self")
            values("self")

            s = lp["self"]

            def tile_self(n, j, first):
                t = 4 * n + j
                sc3 = bank[j][:].rearrange("p (h k) -> p h k", h=4)
                dve.wait_ge(s["scores"], t + 1)
                v.tensor_reduce(nmax[:, j, :], sc3, AX_X, ALU.max).then_inc(s["topped"], 1)
                dve.wait_ge(s["topped"], t + 1)
                if not first:
                    dve.wait_ge(s["p_T"], t - 3)
                v.tensor_tensor(e_buf(j).rearrange("p (h k) -> p h k", h=4), sc3,
                                nmax[:, j, :].unsqueeze(2).broadcast_to([P, 4, P]),
                                ALU.subtract).then_inc(s["scanned"], 1)

            for j in range(4):
                tile_self(0, j, True)
            with dve.Fori(1, NT) as n:
                for j in range(4):
                    tile_self(n, j, False)
            finish("self")
            norm("cross")
            split_parts("cross")
            values("cross")

            s = lp["cross"]

            def tile_cross(n, j, first):
                t = 4 * n + j
                dve.wait_ge(s["scores"], t + 1)
                if not first:
                    dve.wait_ge(s["p_ready"], t - 3)
                dve.sem_inc(turn, 1)
                v.max(top[:, j, 0:8], bank[j][:]).then_inc(s["topped"], 1)
                dve.wait_ge(s["topped"], t + 1)
                dve.sem_inc(turn, 1)
                v.match_replace(s1_buf, top[:, j, 0:8], bank[j][:], TAKEN).then_inc(s["scanned"], 1)
                dve.wait_ge(s["scanned"], t + 1)
                dve.sem_inc(turn, 1)
                v.max(top[:, j, 8:16], s1_buf).then_inc(chain, 1)
                dve.wait_ge(chain, t + 1)
                dve.sem_inc(turn, 1)
                v.match_replace(s2_buf(j), top[:, j, 8:16], s1_buf, TAKEN).then_inc(s["marked"], 1)

            for j in range(4):
                tile_cross(0, j, True)
            with dve.Fori(1, P // 4) as n:
                for j in range(4):
                    tile_cross(n, j, False)
            finish("cross")

            norm("mlp")
            for u in range(2 * 4):
                c, k = divmod(u, 4)
                bcol = COL["L0_xcond_b_m1"] + 4 + k
                dve.wait_ge(mlp["tanh_set"], u + 1)
                v.scalar_tensor_tensor(full_buf(u), rest_buf(u), 1.0, full_buf(u), ALU.add,
                                       ALU.mult).then_inc(mlp["gated"], 1)
                dve.wait_ge(mlp["gated"], u + 1)
                dve.wait_ge(mlp["b_mm"], u + 1)
                if u >= 2:
                    dve.wait_ge(mlp["y_part"], u - 1)
                v.scalar_tensor_tensor(sq_buf(u), bank[2 * (u % 2) + 1][:], cols[:, 0, bcol:bcol + 1], full_buf(u),
                                       ALU.add, ALU.mult).then_inc(mlp["hidden"], 1)
            for c in range(NX):
                dve.wait_ge(mlp["y_set"], c + 1)
                for i in range(2):
                    b = 2 * c + i
                    xb = xT[:, b * L:(b + 1) * L]
                    last = v.scalar_tensor_tensor(xb, xc_buf(c)[:, i * L:(i + 1) * L], mods[:, G_MLP, b:b + 1], xb,
                                                  ALU.mult, ALU.add)
                last.then_inc(mlp["x_new"], 1)

            norm("last")
            split_parts("last")
            values("last")
            s = lp["last"]

            def tile_last(n, j, first, last):
                t = 4 * n + j
                jj = (j - 1) % 4
                if not last:
                    dve.wait_ge(s["scores"], t + 1)
                    if not first:
                        dve.wait_ge(s["expd"], t - 3)
                    v.tensor_reduce(top[:, j, 0:1], bank[j][:], AX_X, ALU.max).then_inc(s["topped"], 1)
                if jj % 2 == 0 and not (first and j == 0):
                    dve.wait_ge(s["p_T"], t)
                    if not (first or (type(n) is int and n == 1 and j == 0)):
                        dve.wait_ge(s["pv"], t - 4)
                    v.tensor_copy(pT_buf(jj), bank[4 + jj % 2][:]).then_inc(s["pT_odd"], 1)

            for n0 in (0, 1):
                for j in range(4):
                    tile_last(n0, j, n0 == 0, False)
            with dve.Fori(2, P // 4) as n:
                for j in range(4):
                    tile_last(n, j, False, False)
            tile_last(P // 4, 0, False, True)
            finish("last")
            dve.wait_ge(out_T, 2)
            v.tensor_copy(tok[:, 4:8, :].rearrange("p t f -> p (t f)"), bank[1][:]).then_inc(out_set[1], 1)

        @block.tensor
        def _(pe):
            t_ = nc.tensor
            mm = t_.matmul
            pe.wait_ge(ident_set, 2)
            pe.wait_ge(vec_in, 16 * (len(VECTORS) + 1))
            pe.wait_ge(vecs_set, 1)
            t_.transpose(bank[7][:, 0:NVEC], vecs[:], ident[0:NVEC, 0:NVEC])
            t_.transpose(bank[7][:, NVEC:2 * NVEC], vecs_p[:],
                         ident[0:NVEC, 0:NVEC]).then_inc(cols_T, 1)
            pe.wait_ge(x_in, 48)
            for t in range(NT):
                last = t_.transpose(bank[t // 4][:, (t % 4) * P:(t % 4 + 1) * P], tok[:, t, :], ident[:])
                if t % 4 == 3:
                    last.then_inc(x_T, 1)
            pe.wait_ge(ctx_in, 16)
            for t in range(NCT):
                last = t_.transpose(bank[2 + t // 4][:, (t % 4) * P:(t % 4 + 1) * P], ctx_tok[:, t, :], ident[:])
                if t % 4 == 3:
                    last.then_inc(ctx_T, 1)
            pe.wait_ge(ada_in, 48)
            pe.wait_ge(silu_set, 1)
            for m in range(NMOD):
                w = w_ada[:, m * C:(m + 1) * C] if m < 9 else w_ss[:, (m - 9) * C:(m - 8) * C]
                last = mm(bank[6][:, m * B:(m + 1) * B], w, silu_c[:], start=True, stop=True)
            last.then_inc(mods_mm, 1)
            pe.wait_ge(ones_set, 2)
            pe.wait_ge(ctxT_set, 4)
            pe.wait_ge(xT_set, 2)

            def norm(stage):
                s = ln
                at = LN_AT[stage]
                src, dst, chunks, eps, sc, sh, per = LN_OF[stage]
                if stage in x_before:
                    pe.wait_ge(*x_before[stage])
                for c0 in range(0, chunks, 2):
                    for c in (c0, c0 + 1):
                        if c >= 2:
                            pe.wait_ge(s["centred"], at + c - 1)
                        mm(bank[2 * (c % 2)][:], mean_w[:], chunk(src, c), start=True,
                           stop=True).then_inc(s["mean_mm"], 1)
                    for c in (c0, c0 + 1):
                        pe.wait_ge(s["squared"], at + c + 1)
                        mm(bank[2 * (c % 2) + 1][:], mean_w[:], sq_buf(c), start=True,
                           stop=True).then_inc(s["var_mm"], 1)

            def project(stage):
                s = sp_
                pe.wait_ge(ln["log_var"], LN_AT[stage] + NX)
                for w, _, src, c, kind, n in units(stage):
                    if src is hT:
                        pe.wait_ge(ln["modulated"], MODULATED_AT[stage] + 2 * (c + 1))
                    if n >= 2:
                        pe.wait_ge(s["full"], n - 1)
                    mm(bank[n % 2][:], w, chunk(src, c), start=True, stop=True).then_inc(s["full_mm"], 1)
                _, w, src, tiles = PROJ[stage]
                for g in range(tiles // 4):
                    if g >= 2:
                        pe.wait_ge(s["v_set"], V_AT[stage] + 4 * (g - 1))
                    for i in range(4):
                        t = 4 * g + i
                        last = mm(bank[2 + g % 2][:, i * C:(i + 1) * C], src[:, t * P:(t + 1) * P], w, start=True,
                                  stop=True)
                    last.then_inc(s["v_mm"], 1)

            def transposes(s, n, j, ready, first):
                t = 4 * n + j
                pe.wait_ge(s[ready], t + 1)
                if not (first and j < 2):
                    if s is lp["last"]:
                        pe.wait_ge(s["pT_odd"] if j % 2 == 0 else s["pT_set"], (4 * n + j) // 2 if type(n) is int else n * 2 + j // 2)
                    else:
                        pe.wait_ge(s["pT_set"], t - 1)
                for i in range(4):
                    last = t_.transpose(bank[4 + j % 2][:, i * P:(i + 1) * P], e_buf(j)[:, i * P:(i + 1) * P], ident[:])
                last.then_inc(s["p_T"], 1)

            def finish(stage):
                s = fin
                w, bcol, vcol, g = OUT[stage]
                for c in range(NX):
                    pe.wait_ge(s["o_norm"], NT * FIN_AT[stage] + 4 * (c + 1))
                    for i in range(4):
                        last = t_.transpose(bank[2 * c][:, i * P:(i + 1) * P], tok[:, 4 * c + i, :], ident[:])
                    last.then_inc(s["o_T"], 1)
                for c in range(NX):
                    pe.wait_ge(s["oT_set"], NX * FIN_AT[stage] + c + 1)
                    mm(bank[2 * c + 1][:], w, chunk(hT, c), start=True, stop=True).then_inc(s["y_mm"], 1)

            def wait_stacked(stage):
                for n in [u[-1] for u in units(stage)][-2:]:
                    pe.wait_ge(sp_[f"stacked{n % 2}"], stacked_after[n])

            norm("ctx")
            norm("self")
            pe.wait_ge(w_in, 160)
            pe.wait_ge(w_qk_set, 6)
            project("self")
            pe.wait_ge(sp_["v_set"], V_AT["self"] + NT)
            pe.wait_ge(win_in, 16 * 2 * H)
            wait_stacked("self")

            s = lp["self"]

            def scores_self(n, j, first):
                t = 4 * n + j
                if not first:
                    pe.wait_ge(s["scanned"], t - 3)
                at = (n // 2) * (H * L) + (n % 2) * P
                for i in range(4):
                    h = 4 * j + i
                    last = mm(bank[j][:, i * P:(i + 1) * P], q_stack[:, bass.ds(at + h * L, P)],
                              k_stack[:, bass.ds(at + h * L, P)], start=True, stop=True)
                last.then_inc(s["scores"], 1)

            def pv_self(n, j, first):
                t = 4 * n + j
                pe.wait_ge(s["pT_set"], t + 1)
                if j == 0 and not first:
                    pe.wait_ge(s["o_set"], n)
                for i in range(4):
                    h = 4 * j + i
                    last = mm(bank[O_BANK][:, h * DV:(h + 1) * DV], pT_buf(j)[:, i * P:(i + 1) * P],
                              v_self[:].rearrange("p t h e -> p (t h e)")[:, bass.ds(n * (H * DV) + h * DV, DV)],
                              start=True, stop=True)
                last.then_inc(s["pv"], 1)

            def attend(s, N, scores, pv, ready):
                def body(n, first, last):
                    for j in range(4):
                        if j < 2:
                            scores(n, j + 2, first)
                        elif not last:
                            scores(n + 1, j - 2, False)
                        if j >= 1:
                            transposes(s, n, j - 1, ready, first)
                        elif not first:
                            transposes(s, n - 1, 3, ready, type(n) is int and n == 0)
                        if j >= 2:
                            pv(n, j - 2, first)
                        elif not first:
                            pv(n - 1, j + 2, type(n) is int and n == 1)
                scores(0, 0, True)
                scores(0, 1, True)
                body(0, True, False)
                with pe.Fori(1, N - 1) as n:
                    body(n, False, False)
                body(N - 1, False, True)
                transposes(s, N - 1, 3, ready, False)
                pv(N - 1, 2, False)
                pv(N - 1, 3, False)

            attend(s, NT, scores_self, pv_self, "expd")
            finish("self")
            norm("cross")
            project("cross")
            pe.wait_ge(sp_["v_set"], V_AT["cross"] + NCT)
            wait_stacked("cross")

            def scores_ctx(s, frees):
                def f(n, j, first):
                    t = 4 * n + j
                    if not first:
                        for name in frees:
                            pe.wait_ge(s[name], t - 3)
                    g = 2 * n + j // 2
                    mm(bank[j][:], q_stack[0:KS, bass.ds(g * L + (j % 2) * P, P)], k_stack[0:KS, bass.ds(g * LC, LC)],
                       start=True, stop=True).then_inc(s["scores"], 1)
                return f

            def pv_ctx(s):
                def f(n, j, first):
                    t = 4 * n + j
                    if s is lp["last"]:
                        pe.wait_ge(s["pT_odd"] if j % 2 == 0 else s["pT_set"], n * 2 + j // 2 + 1)
                    else:
                        pe.wait_ge(s["pT_set"], t + 1)
                    if j == 0 and not first:
                        pe.wait_ge(s["o_set"], n)
                    vf = v_ctx[:].rearrange("p b h c e -> p (b h c e)")
                    g = 2 * n + j // 2
                    for c in range(KC):
                        last = mm(bank[O_BANK][:, j * DV:(j + 1) * DV], pT_buf(j)[:, c * P:(c + 1) * P],
                                  vf[:, bass.ds(g * (KC * DV) + c * DV, DV)], start=(c == 0), stop=(c == KC - 1))
                    last.then_inc(s["pv"], 1)
                return f

            s = lp["cross"]
            attend(s, P // 4, scores_ctx(s, ("expd",)), pv_ctx(s), "p_ready")
            finish("cross")

            norm("mlp")
            pe.wait_ge(ln["modulated"], MODULATED_AT["mlp"] + 4)

            def down(u):
                c, k = divmod(u, 4)
                pe.wait_ge(mlp["hidden"], u + 1)
                last = mm(bank[4 + c][:], w_m2[:, k, :], sq_buf(u), start=(k == 0), stop=(k == 3))
                last.then_inc(mlp["y_part"], 1)

            for u in range(2 * 4):
                c, k = divmod(u, 4)
                if u >= 2:
                    pe.wait_ge(mlp["tanh_set"], u - 1)
                mm(bank[2 * (u % 2)][:], w_m1[:, k * P:(k + 1) * P], chunk(hT, c), start=True,
                   stop=True).then_inc(mlp["a_mm"], 1)
                if u >= 2:
                    down(u - 2)
                mm(bank[2 * (u % 2) + 1][:], w_m1[:, HID + k * P:HID + (k + 1) * P], chunk(hT, c), start=True,
                   stop=True).then_inc(mlp["b_mm"], 1)
            down(6)
            down(7)

            norm("last")
            project("last")
            pe.wait_ge(sp_["v_set"], V_AT["last"] + NCT)
            wait_stacked("last")
            s = lp["last"]
            attend(s, P // 4, scores_ctx(s, ("expd",)), pv_ctx(s), "expd")
            finish("last")
            for c in range(NX):
                pe.wait_ge(fin["x_new"], 2 * NX + c + 1)
                for i in range(4):
                    t = 4 * c + i
                    last = t_.transpose(bank[c][:, i * P:(i + 1) * P], xT[:, t * P:(t + 1) * P], ident[:])
                last.then_inc(out_T, 1)


_OUT_SHAPE = (B, L, C)


def kernel(**inputs):
    import numpy as _np
    import concourse.bacc as _bacc
    from concourse.bass_utils import run_bass_kernel_spmd as _run

    nc = _bacc.Bacc("TRN2", target_bir_lowering=False, num_devices=1)
    arrays, args = {}, {}
    for name, value in inputs.items():
        value = _np.ascontiguousarray(value)
        arrays[f"in_{name}"] = value
        args[name] = nc.dram_tensor(f"in_{name}", value.shape, mybir.dt.from_np(value.dtype), kind="ExternalInput").ap()
    out = nc.dram_tensor("out", _OUT_SHAPE, F32, kind="ExternalOutput").ap()
    pixart_kernel(nc, args, out)
    r = _run(nc, [arrays], core_ids=[0])
    return r.results[0]["out"]
```

```python
from contextlib import ExitStack

import concourse.bass as bass
from concourse import mybir

F32 = mybir.dt.float32
BF16 = mybir.dt.bfloat16
F16 = mybir.dt.float16
ALU = mybir.AluOpType
ACT = mybir.ActivationFunctionType
AX_X = mybir.AxisListType.X

P = 128
B, L, LC, C = 4, 256, 512, 128
H = 16
D = C // H
HID = 512
WIN, SHIFT = 64, 32
EPS0, EPS1 = 1e-6, 1e-5
SCALE = float(D) ** -0.5
TAKEN = -3.0e38
OFF_WINDOW = -1.0e30

NTOK = B * L
NCTX = B * LC
NT = NTOK // P
NCT = NCTX // P
CH = 512
NX = NTOK // CH
KC = LC // P
DV = D + 1

Q_PART = (0, 0, 0, 1, 1, 2)
K_PART = (0, 1, 2, 0, 1, 0)
KS = D * len(Q_PART)
W_UP = 4096.0
VP = 3 * DV

VECTORS = (
    ("L0_xcond_b_ada", 9), ("L1_xcond_bss_q", 2), ("L1_xcond_bss_kv", 2), ("L0_xcond_b_qkv", 3),
    ("L0_xcond_b_so", 1), ("L0_xcond_b_q", 1), ("L0_xcond_b_kv", 2), ("L0_xcond_b_co", 1),
    ("L0_xcond_b_m1", 8), ("L0_xcond_b_m2", 1), ("L1_xcond_bq", 1), ("L1_xcond_bkv", 2),
    ("L1_xcond_bp", 1),
)
COL = {}
_at = 0
for _name, _rows in VECTORS:
    COL[_name] = _at
    _at += _rows
COND_AT = _at
NVEC = _at + B
NMOD = 13
SH_MSA, SC_MSA, G_MSA, SH_MCA, SC_MCA, G_MCA, SH_MLP, SC_MLP, G_MLP, SC_Q, SH_Q, SC_KV, SH_KV = range(NMOD)


def pixart_kernel(nc, a, out):
    with ExitStack() as ctx:
        def sb(name, shape, dt=F32):
            return ctx.enter_context(nc.sbuf_tensor(name, shape, dt))

        def sem(name):
            return ctx.enter_context(nc.semaphore(name))

        ident = sb("ident", [P, P])
        mean_w = sb("mean_w", [P, P])
        neg_scale = sb("neg_scale", [P, 1])
        vecs = sb("vecs", [NVEC, P])
        vecs_p = sb("vecs_p", [NVEC, P])
        w_qk = sb("w_qk", [P, 6, C])
        cols = sb("cols", [P, 2, NVEC])
        half_b1 = sb("half_b1", [P, 4])
        w_qkv = sb("w_qkv", [P, 3 * C])
        w_so = sb("w_so", [P, C])
        w_q = sb("w_q", [P, C])
        w_kv = sb("w_kv", [P, 2 * C])
        w_co = sb("w_co", [P, C])
        w_m1 = sb("w_m1", [P, 2 * HID])
        w_m2 = sb("w_m2", [P, HID // P, C])
        w1_q = sb("w1_q", [P, C])
        w1_kv = sb("w1_kv", [P, 2 * C])
        w1_p = sb("w1_p", [P, C])
        silu_c = sb("silu_c", [P, B])
        silu_e = sb("silu_e", [P, B])
        mods = sb("mods", [P, NMOD, B])
        tok = sb("tok", [P, NT, P])
        xT = sb("xT", [P, NTOK])
        ctxT = sb("ctxT", [P, NCTX])
        q_stack = sb("q_stack", [KS + 2, H * NTOK], BF16)
        k_all = sb("k_all", [P, H * NCTX], BF16)
        k_stack = k_all[0:KS + 2, :]
        k_late = k_all[:, H * NTOK:].bitcast(F32)
        ctx_tok = k_late[:, 0:NCTX].rearrange("p (t f) -> p t f", f=P)
        w_ada = k_late[:, NCTX:NCTX + 9 * C]
        w_ss = k_late[:, NCTX + 9 * C:NCTX + 13 * C]
        v_self = sb("v_self", [P, NT, H, VP], BF16)
        v_all = sb("v_all", [P, H * B * KC * VP], BF16)
        v_ctx = v_all[:, 0:2 * H * B * KC * DV].bitcast(F32).rearrange("p (h b c e) -> p h b c e", h=H, b=B, c=KC)
        v_last = v_all[:].rearrange("p (h b c e) -> p h b c e", h=H, b=B, c=KC)
        o_raw = sb("o_raw", [P, H, NT, DV])
        windows = o_raw[0:2].rearrange("p h t e -> p (h t e)").bitcast(BF16)
        winq, wink = windows[:, 0:NTOK], windows[:, NTOK:2 * NTOK]
        rden = sb("rden", [P, H, NT])
        o9 = sb("o9", [DV, CH])
        top = sb("top", [P, 4, 16])
        nmax = sb("nmax", [P, 4, 4])
        parts_own = sb("parts_own", [P, 2, 3, 2 * CH], BF16)
        work = sb("work", [P, 14, CH])
        v_stage = sb("v_stage", [P, 4, KC * DV])
        v_stage3 = sb("v_stage3", [P, 4, 4 * VP], BF16)

        def e_buf(j):
            return work[:, j, :]

        pT_pair = work[:, 4:8, :]

        def pT_buf(j):
            return work[:, 4 + j, :]

        def pT_part(j, i):
            return pT_buf(j).bitcast(F16)[:, i * CH:(i + 1) * CH]

        def s2_buf(j):
            return work[:, 8 + j, :]

        def s1_buf(j):
            return work[:, 12 + j % 2, :]

        def xc_buf(c):
            return work[:, c % 2, :]

        def sq_buf(c):
            return work[:, 2 + c % 2, :]

        hT = work[:, 4:6, :].rearrange("p c n -> p (c n)")

        def full_buf(i):
            return work[:, 6 + i % 2, :]

        def rest_buf(i):
            return sq_buf(i)

        def tanh_buf(u):
            return work[:, 8 + u % 2, :]

        parts_work = work[:, 8:14, :].rearrange("p a n -> p (a n)").bitcast(BF16).rearrange(
            "p (r s n) -> p r s n", r=2, s=3)

        def pair_parts(pair):
            return parts_work[:, pair - 2] if pair in (2, 3) else parts_own[:, (0, 1, 0, 0, 0, 1, 0, 1)[pair]]

        def part_buf(n, i):
            return pair_parts(n // 2)[:, i, (n % 2) * CH:(n % 2 + 1) * CH]

        BUFFER_AFTER = {4: 0, 5: 1, 6: 4, 7: 5}

        bank = [ctx.enter_context(nc.psum_tensor(f"bank{i}", [P, 512], F32)) for i in range(8)]
        O_BANK, BACK_BANK = 6, 7

        def unit_bank(n):
            return bank[4 + n % 2]

        def v_bank(g):
            return bank[6 + g % 2]

        ones_set = sem("ones_set")
        ident_set = sem("ident_set")
        win_set = sem("win_set")
        vec_in = sem("vec_in")
        x_in = sem("x_in")
        ctx_in = sem("ctx_in")
        ada_in = sem("ada_in")
        w_in = sem("w_in")
        win_in = sem("win_in")
        cols_T = sem("cols_T")
        cols_set = sem("cols_set")
        vecs_set = sem("vecs_set")
        w_qk_set = sem("w_qk_set")
        cond_step = sem("cond_step")
        silu_exp = sem("silu_exp")
        silu_set = sem("silu_set")
        mods_mm = sem("mods_mm")
        mods_set = sem("mods_set")
        x_T = sem("x_T")
        xT_set = sem("xT_set")
        ctx_T = sem("ctx_T")
        ctxT_set = sem("ctxT_set")
        out_T = sem("out_T")
        out_set = [sem(f"out_set{c}") for c in range(NX)]
        stored = sem("stored")

        def stage_sems(names, stage):
            return {n: sem(f"{n}_{stage}") for n in names}

        ln = stage_sems(("mean_mm", "centred", "squared", "var_mm", "log_var", "rstd", "normed", "modulated"), "norm")
        LN_AT = {"self": 0, "ctx": NX, "cross": NX + B, "mlp": 2 * NX + B, "last": 3 * NX + B}
        MODULATED_AT = {"self": 0, "ctx": B, "cross": 2 * B, "mlp": 3 * B, "last": 4 * B}
        split = stage_sems(("full_mm", "full", "part0", "rest", "part1", "part2"), "split")
        stacked = [sem(f"stacked{i}") for i in range(8)]
        vals = stage_sems(("mm", "part0", "rest", "set"), "v")
        fin = stage_sems(("recip", "o_norm", "o_T", "oT_set", "y_mm", "y_set", "x_new"), "out")
        FIN_AT = {"self": 0, "cross": 1, "last": 2}
        lp = {
            "self": stage_sems(("scores", "topped", "scanned", "expd", "p_T", "pT_set", "rest_set", "pv", "o_set"), "self"),
            "cross": stage_sems(("scores", "topped", "nm", "scanned", "expd", "marked", "masked", "p_ready", "p_T",
                                 "pT_set", "pv", "o9_set", "back_T", "o_set"), "cross"),
            "last": stage_sems(("scores", "topped", "nm", "expd", "p_T", "pT_set", "rest_set", "pv", "o_set"), "last"),
        }
        for _s in lp:
            lp[_s]["staged"] = sem(f"staged_{_s}")
        chain = sem("chain")
        turn = sem("turn")
        pool_turn = sem("pool_turn")
        pe_turn = sem("pe_turn")
        mlp = stage_sems(("a_mm", "b_mm", "a_set", "tanh_set", "gated", "hidden", "y_part", "y_set", "x_new"), "mlp")

        x_before = {"self": (xT_set, 2), "cross": (fin["x_new"], NX), "mlp": (fin["x_new"], 2 * NX),
                    "last": (mlp["x_new"], NX)}
        LN_OF = {
            "self": (xT, hT, NX, EPS0, SC_MSA, SH_MSA, 2),
            "cross": (xT, hT, NX, EPS0, SC_MCA, SH_MCA, 2),
            "mlp": (xT, hT, NX, EPS0, SC_MLP, SH_MLP, 2),
            "last": (xT, hT, NX, EPS1, SC_Q, SH_Q, 2),
            "ctx": (ctxT, ctxT, B, EPS1, SC_KV, SH_KV, 1),
        }

        def chunk(t, c):
            return t[:, c * CH:(c + 1) * CH]

        bqkv, bkv, b1kv = COL["L0_xcond_b_qkv"], COL["L0_xcond_b_kv"], COL["L1_xcond_bkv"]
        UNITS = (
            [(w_qk[:, 0, :], bqkv, hT, c) for c in range(NX)]
            + [(w_qk[:, 1, :], bqkv + 1, hT, c) for c in range(NX)]
            + [(w_qk[:, 3, :], bkv, ctxT, c) for c in range(B)]
            + [(w_qk[:, 2, :], COL["L0_xcond_b_q"], hT, c) for c in range(NX)]
            + [(w_qk[:, 5, :], b1kv, ctxT, c) for c in range(B)]
            + [(w_qk[:, 4, :], COL["L1_xcond_bq"], hT, c) for c in range(NX)]
        )
        SELF_QK, CROSS_K, CROSS_Q, LAST_K, LAST_Q = (0, 4), (4, 8), (8, 10), (10, 14), (14, 16)
        UNITS_BEFORE = {"self": 0, "ctx": 8, "cross": 8, "mlp": 14, "last": 14}
        VALUES = {
            "self": (w_qkv[:, 2 * C:3 * C], hT, 0, NT // 4),
            "cross": (w_kv[:, C:2 * C], ctxT, 2, B),
            "last": (w1_kv[:, C:2 * C], ctxT, 6, B),
        }
        OUT = {
            "self": (w_so[:], COL["L0_xcond_b_so"], bqkv + 2, G_MSA),
            "cross": (w_co[:], COL["L0_xcond_b_co"], bkv + 1, G_MCA),
            "last": (w1_p[:], COL["L1_xcond_bp"], b1kv + 1, None),
        }

        v_copied = sem("v_copied")
        v_read = sem("v_read")

        def v_number(g0, i):
            return i + (0 if g0 == 0 else 2)

        def v_dst(stage, i, part):
            e = slice(part * DV, part * DV + D)
            if stage == "self":
                return v_self[:, 4 * i:4 * i + 4, :, e]
            return v_last[:, :, i, :, e].rearrange("p h c e -> p c h e")

        block = ctx.enter_context(nc.Block())

        @block.sync
        def _(sp):
            for name, rows in VECTORS:
                at = COL[name]
                sp.dma_start(vecs[at:at + rows, :], a[name].rearrange("(r n) -> r n", n=P)).then_inc(vec_in, 16)
            sp.dma_start(vecs[COND_AT:NVEC, :], a["cond_1024"]).then_inc(vec_in, 16)
            x = a["x"]
            tiles = tok[:].rearrange("p (b h) f -> p b h f", h=2)
            sp.dma_start(tiles[:, :, 0, :], x[:, SHIFT:SHIFT + P, :].rearrange("b p f -> p b f")).then_inc(x_in, 16)
            sp.dma_start(tiles[0:P - SHIFT, :, 1, :],
                         x[:, SHIFT + P:L, :].rearrange("b p f -> p b f")).then_inc(x_in, 16)
            sp.dma_start(tiles[P - SHIFT:P, :, 1, :],
                         x[:, 0:SHIFT, :].rearrange("b p f -> p b f")).then_inc(x_in, 16)
            sp.wait_ge(win_set, 3)
            for stack, rows in ((q_stack[:], winq), (k_stack, wink)):
                sp.dma_start(stack[KS:KS + 2, 0:H * NTOK].rearrange("r (h n) -> r h n", h=H),
                             rows.unsqueeze(1).broadcast_to([2, H, NTOK])).then_inc(win_in, 16)

            def stack(pair, kind):
                parts = pair_parts(pair)
                if kind == "k":
                    k0 = 2 * (UNITS[2 * pair][3] // 2)
                    dst = k_stack.rearrange("r (h b n) -> r h b n", h=H, b=B)[:, :, k0:k0 + 2, :].rearrange(
                        "r h b n -> r h (b n)")
                else:
                    dst = (q_stack[:] if kind == "q" else k_stack)[:, 0:H * NTOK].rearrange("r (h n) -> r h n", h=H)
                for t, part in enumerate(Q_PART if kind == "q" else K_PART):
                    sp.wait_ge(split[f"part{part}"], 2 * pair + 2)
                    sp.dma_start(dst[D * t:D * t + D], parts[:, part, :]).then_inc(stacked[pair], 16)

            stack(0, "q")
            stack(1, "self k")
            sp.wait_ge(lp["self"]["scores"], NT * 4)
            stack(2, "k")
            stack(3, "k")
            stack(4, "q")
            sp.wait_ge(lp["cross"]["scores"], P)
            stack(5, "k")
            stack(6, "k")
            stack(7, "q")
            for t in range(NT):
                b, half = divmod(t, 2)
                if half == 0:
                    sp.wait_ge(out_set[t // 4], 1)
                    sp.dma_start(out[b, SHIFT:SHIFT + P, :], tok[:, t, :]).then_inc(stored, 16)
                else:
                    sp.dma_start(out[b, SHIFT + P:L, :], tok[0:P - SHIFT, t, :]).then_inc(stored, 16)
                    sp.dma_start(out[b, 0:SHIFT, :], tok[P - SHIFT:P, t, :]).then_inc(stored, 16)
            sp.wait_ge(stored, 16 * 3 * B)

        @block.gpsimd
        def _(pool):
            g = nc.gpsimd
            g.memset(ident[:], 0.0).then_inc(ident_set, 1)
            g.memset(neg_scale[:], -SCALE).then_inc(ones_set, 1)
            g.memset(mean_w[:], 1.0 / C).then_inc(ones_set, 1)
            pool.wait_ge(ident_set, 1)
            g.affine_select(out=ident[:], in_=ident[:], compare_op=ALU.not_equal, fill=1.0, base=0,
                            pattern=[[-1, P]], channel_multiplier=1).then_inc(ident_set, 1)
            g.memset(winq, 1.0).then_inc(win_set, 1)
            pool.wait_ge(win_set, 1)
            wq = winq.rearrange("r (t w n) -> r t w n", w=2, n=WIN)
            g.affine_select(out=wq, in_=wq, compare_op=ALU.is_equal, fill=0.0, base=0,
                            pattern=[[0, NT], [-1, 2], [0, WIN]], channel_multiplier=1).then_inc(win_set, 1)
            pool.wait_ge(win_set, 2)
            g.tensor_scalar(wink, winq, -OFF_WINDOW, OFF_WINDOW, ALU.mult, ALU.add).then_inc(win_set, 1)
            pool.dma_start(w_ada, a["L0_xcond_w_ada"]).then_inc(ada_in, 16)
            pool.dma_start(w_ss[:, 0:2 * C], a["L1_xcond_Wss_q"]).then_inc(ada_in, 16)
            pool.dma_start(w_ss[:, 2 * C:], a["L1_xcond_Wss_kv"]).then_inc(ada_in, 16)
            g.memset(v_self[:, :, :, D:VP], 0.0).then_inc(ones_set, 1)
            g.memset(v_ctx[:, :, :, :, D:DV], 1.0).then_inc(ones_set, 1)
            pool.wait_ge(ones_set, 4)
            g.memset(v_self[:, :, :, D:DV], 1.0).then_inc(ones_set, 1)
            pool.wait_ge(w_in, 160)
            for i, w in enumerate((w_qkv[:, 0:C], w_qkv[:, C:2 * C], w_q[:], w_kv[:, 0:C], w1_q[:], w1_kv[:, 0:C])):
                g.tensor_copy(w_qk[:, i, :].rearrange("p (d h) -> p d h", h=H),
                              w.rearrange("p (h d) -> p d h", h=H)).then_inc(w_qk_set, 1)

            def last_parts(first, end):
                for n in range(first, end):
                    pool.wait_ge(split["part1"], n + 1)
                    g.tensor_tensor(part_buf(n, 2), rest_buf(n), part_buf(n, 1), ALU.subtract).then_inc(
                        split["part2"], 1)

            def last_v_parts(stage):
                _, _, g0, groups = VALUES[stage]
                for i in range(groups):
                    pool.wait_ge(vals["rest"], v_number(g0, i) + 1)
                    g.tensor_tensor(v_dst(stage, i, 2), xc_buf(i).rearrange("p (t h d) -> p t h d", t=4, h=H),
                                    v_dst(stage, i, 1), ALU.subtract).then_inc(vals["set"], 1)

            def stage_self(n, p, first):
                s = lp["self"]
                vf = v_self[:].rearrange("p t h e -> p (t h e)")
                for j in (2 * p, 2 * p + 1):
                    if not first:
                        pool.wait_ge(s["pv"], 4 * n + j - 3)
                    pool.sem_inc(pool_turn, 1)
                    g.tensor_copy(v_stage3[:, j, :], vf[:, bass.ds(n * (H * VP) + j * (4 * VP), 4 * VP)]).then_inc(
                        s["staged"], 1)

            def stage_ctx(stage):
                s = lp[stage]
                cross = stage == "cross"
                vf = (v_ctx if cross else v_last).rearrange("p h b c e -> p (h b c e)")
                to = v_stage if cross else v_stage3
                w = KC * (DV if cross else VP)

                def f(n, p, first):
                    if not first:
                        pool.wait_ge(s["pv"], 4 * n + 2 * p - 2)
                    pool.sem_inc(pool_turn, 1)
                    g.tensor_copy(to[:, 2 * p, :], vf[:, bass.ds((2 * n + p) * w, w)]).then_inc(s["staged"], 1)
                return f

            def negate(s, t, j):
                pool.wait_ge(s["topped"], t + 1)
                g.tensor_tensor(nmax[:, j, 0:1], top[:, j, 0:1], neg_scale[:], ALU.mult).then_inc(s["nm"], 1)

            def take(s, t, j):
                pool.wait_ge(s["masked"], t + 1)
                g.tensor_tensor(e_buf(j), e_buf(j), s2_buf(j), ALU.subtract).then_inc(s["p_ready"], 1)

            def body_self(n, p, first, last):
                if p == 1:
                    if not last:
                        stage_self(n, 0, first)
                elif not first:
                    stage_self(n - 1, 1, type(n) is int and n == 1)

            def body_cross(n, p, first, last):
                stage, s = "cross", lp["cross"]
                t, j = 4 * n + 2 * p, 2 * p
                before = not (first and p == 0)
                if before:
                    take(s, t - 2, (j - 2) % 4)
                if not last:
                    negate(s, t, j)
                    negate(s, t + 1, j + 1)
                if before:
                    take(s, t - 1, (j - 1) % 4)
                if p == 1:
                    stage_ctx(stage)(n, 0, first)
                elif before:
                    stage_ctx(stage)(n - 1, 1, type(n) is int and n == 1)

            def body_last(n, p, first, last):
                stage, s = "last", lp["last"]
                if not last:
                    negate(s, 4 * n + 2 * p, 2 * p)
                    negate(s, 4 * n + 2 * p + 1, 2 * p + 1)
                if p == 1:
                    stage_ctx(stage)(n, 0, first)
                elif not first:
                    stage_ctx(stage)(n - 1, 1, type(n) is int and n == 1)

            def run(N, body):
                for n0 in (0, 1):
                    for p in (0, 1):
                        body(n0, p, n0 == 0, False)
                with pool.Fori(2, N) as n:
                    for p in (0, 1):
                        body(n, p, False, False)
                body(N, 0, False, True)

            last_parts(*SELF_QK)
            last_v_parts("self")
            last_parts(*CROSS_K)
            pool.wait_ge(v_copied, B)
            run(NT, body_self)
            last_parts(*CROSS_Q)
            run(P // 4, body_cross)
            pool.wait_ge(lp["cross"]["staged"], H * B)
            g.memset(v_last[:, :, :, :, D:VP], 0.0).then_inc(ones_set, 1)
            pool.wait_ge(ones_set, 6)
            g.memset(v_last[:, :, :, :, D:DV], 1.0).then_inc(ones_set, 1)
            last_parts(*LAST_K)
            last_v_parts("last")
            last_parts(*LAST_Q)
            run(P // 4, body_last)

        @block.scalar
        def _(act):
            s_ = nc.scalar
            act.dma_start(ctx_tok, a["ctx_1024"].rearrange("b (c p) f -> p (b c) f", p=P)).then_inc(ctx_in, 16)
            for dst, name in ((w_qkv[:], "L0_xcond_w_qkv"), (w_so[:], "L0_xcond_w_so"), (w_q[:], "L0_xcond_w_q"),
                              (w_kv[:], "L0_xcond_w_kv"), (w_co[:], "L0_xcond_w_co"), (w_m1[:], "L0_xcond_w_m1"),
                              (w1_q[:], "L1_xcond_Wq"), (w1_kv[:], "L1_xcond_Wkv"), (w1_p[:], "L1_xcond_Wp")):
                act.dma_start(dst, a[name]).then_inc(w_in, 16)
            act.dma_start(w_m2[:], a["L0_xcond_w_m2"].rearrange("(k p) n -> p k n", p=P)).then_inc(w_in, 16)
            act.wait_ge(cols_set, 1)
            s_.activation(silu_e[:], cols[:, 0, COND_AT:NVEC], ACT.Exp, scale=-1.0).then_inc(silu_exp, 1)
            act.wait_ge(x_T, 1)
            s_.activation(chunk(xT, 0), bank[0][:], ACT.Copy).then_inc(xT_set, 1)
            def norm(stage):
                s = ln
                at = LN_AT[stage]
                src, dst, chunks, eps, sc, sh, per = LN_OF[stage]
                if UNITS_BEFORE[stage]:
                    act.wait_ge(split["part2"], UNITS_BEFORE[stage])
                for c0 in range(0, chunks, 2):
                    for c in (c0, c0 + 1):
                        if c >= 2:
                            act.wait_ge(s["normed"], at + c - 1)
                        act.wait_ge(s["centred"], at + c + 1)
                        s_.activation(sq_buf(c), xc_buf(c), ACT.Square).then_inc(s["squared"], 1)
                    for c in (c0, c0 + 1):
                        act.wait_ge(s["var_mm"], at + c + 1)
                        s_.activation(sq_buf(c), bank[2 * (c % 2) + 1][:], ACT.Ln, bias=eps).then_inc(s["log_var"], 1)
                    for c in (c0, c0 + 1):
                        act.wait_ge(s["log_var"], at + c + 1)
                        s_.activation(sq_buf(c), sq_buf(c), ACT.Exp, scale=-0.5).then_inc(s["rstd"], 1)
                    for c in (c0, c0 + 1):
                        act.wait_ge(s["normed"], at + c + 1)
                        if stage == "self" and c == 0:
                            act.wait_ge(mods_set, 2)
                        if stage == "ctx" and c == 0:
                            act.wait_ge(split["full_mm"], CROSS_K[1])
                            act.wait_ge(vals["mm"], 2 + B)
                        for i in range(per):
                            b = c * per + i
                            n = CH // per
                            s_.activation(dst[:, b * n:(b + 1) * n], xc_buf(c)[:, i * n:(i + 1) * n], ACT.Identity,
                                          scale=mods[:, sc, b:b + 1], bias=mods[:, sh, b:b + 1]).then_inc(
                                s["modulated"], 1)

            def fulls(first, end):
                for n in range(first, end):
                    col = UNITS[n][1]
                    act.wait_ge(split["full_mm"], n + 1)
                    if n >= 2:
                        act.wait_ge(split["rest"], n - 1)
                    s_.activation(full_buf(n), unit_bank(n)[:], ACT.Identity,
                                  bias=cols[:, 1, col:col + 1]).then_inc(split["full"], 1)

            def first_v_parts(stage):
                _, _, g0, groups = VALUES[stage]
                for i in range(groups):
                    act.wait_ge(vals["mm"], g0 + i + 1)
                    if i == 0:
                        act.wait_ge(ones_set, 7 if stage == "last" else 5)
                    s_.activation(v_dst(stage, i, 0), v_bank(g0 + i)[:].rearrange("p (t h d) -> p t h d", t=4, h=H),
                                  ACT.Copy).then_inc(vals["part0"], 1)

            def finish(stage):
                s = fin
                w, bcol, vcol, g = OUT[stage]
                for c in range(NX):
                    act.wait_ge(s["o_T"], NX * FIN_AT[stage] + c + 1)
                    s_.activation(chunk(hT, c), bank[2 * c][:], ACT.Identity,
                                  bias=cols[:, 0, vcol:vcol + 1]).then_inc(s["oT_set"], 1)
                if stage == "cross":
                    act.wait_ge(vals["set"], 2 + B)
                for c in range(NX):
                    act.wait_ge(s["y_mm"], NX * FIN_AT[stage] + c + 1)
                    s_.activation(xc_buf(c), bank[2 * c + 1][:], ACT.Identity,
                                  bias=cols[:, 0, bcol:bcol + 1]).then_inc(s["y_set"], 1)

            norm("self")
            fulls(*SELF_QK)
            first_v_parts("self")
            for c in (0, 2):
                act.wait_ge(ctx_T, c + 1)
                s_.activation(chunk(ctxT, c), bank[c][:], ACT.Copy).then_inc(ctxT_set, 1)
            fulls(*CROSS_K)
            norm("ctx")

            s = lp["self"]
            N = NT

            def halves(s, t, j, wait_pv):
                act.wait_ge(s["p_T"], t + 1)
                if wait_pv:
                    act.wait_ge(s["pv"], t - 3)
                s_.activation(pT_part(j, 0), bank[4 + j % 2][:], ACT.Copy, scale=W_UP).then_inc(s["pT_set"], 1)

            def body_self(n, p, first, last):
                t, j = 4 * n + 2 * p, 2 * p
                if not first:
                    for i in (0, 1):
                        halves(s, t - 4 + i, j + i, not (type(n) is int and n == 1))
                if not last:
                    for i in (0, 1):
                        act.wait_ge(s["scanned"], t + i + 1)
                        s_.activation(e_buf(j + i), e_buf(j + i), ACT.Exp, scale=SCALE).then_inc(s["expd"], 1)

            def run(N, body):
                for n0 in (0, 1):
                    for p in (0, 1):
                        body(n0, p, n0 == 0, False)
                with act.Fori(2, N) as n:
                    for p in (0, 1):
                        body(n, p, False, False)
                body(N, 0, False, True)

            run(NT, body_self)
            for i in (0, 1):
                halves(s, 4 * NT - 2 + i, 2 + i, True)
            finish("self")
            norm("cross")
            fulls(*CROSS_Q)

            s = lp["cross"]
            N = P // 4

            def leave(s, t, j, wait_pv):
                act.wait_ge(s["p_T"], t + 1)
                if wait_pv:
                    act.wait_ge(s["pv"], t - 3)
                s_.activation(pT_buf(j), bank[4 + j % 2][:], ACT.Copy).then_inc(s["pT_set"], 1)

            def rows_out(n):
                act.wait_ge(s["pv"], 4 * n + 4)
                s_.activation(o9[:], bank[O_BANK][0:DV, :], ACT.Copy).then_inc(s["o9_set"], 1)

            def back_out(n):
                act.wait_ge(s["back_T"], n + 1)
                dst = o_raw[:].rearrange("p h t e -> p (h t e)")
                s_.activation(dst[:, bass.ds(n * (4 * DV), 4 * DV)], bank[BACK_BANK][:, 0:4 * DV],
                              ACT.Copy).then_inc(s["o_set"], 1)

            def body_cross(n, p, first, last):
                t, j = 4 * n + 2 * p, 2 * p
                if not (first and p == 0):
                    for i in (0, 1):
                        jj = (j - 2 + i) % 4
                        act.wait_ge(s["marked"], t - 1 + i)
                        s_.activation(s2_buf(jj), s2_buf(jj), ACT.Exp, scale=SCALE,
                                      bias=nmax[:, jj, 0:1]).then_inc(s["masked"], 1)
                if not first:
                    for i in (0, 1):
                        leave(s, t - 4 + i, j + i, not (type(n) is int and n == 1))
                    if not (type(n) is int and n == 1):
                        rows_out(n - 2) if p == 0 else back_out(n - 2)
                if not last:
                    for i in (0, 1):
                        act.wait_ge(s["nm"], t + i + 1)
                        act.wait_ge(s["scanned"], t + i + 1)
                        if not first:
                            act.wait_ge(s["p_T"], t + i - 3)
                        s_.activation(e_buf(j + i), bank[j + i][:], ACT.Exp, scale=SCALE,
                                      bias=nmax[:, j + i, 0:1]).then_inc(s["expd"], 1)

            run(N, body_cross)
            back_out(N - 2)
            for i in (0, 1):
                leave(s, 4 * N - 2 + i, 2 + i, True)
            rows_out(N - 1)
            back_out(N - 1)
            fulls(*LAST_K)
            first_v_parts("last")
            finish("cross")

            norm("mlp")
            for u in range(2 * 4):
                c, k = divmod(u, 4)
                bcol = COL["L0_xcond_b_m1"] + k
                act.wait_ge(mlp["a_mm"], u + 1)
                if u >= 2:
                    act.wait_ge(mlp["hidden"], u - 1)
                s_.activation(full_buf(u), bank[2 * (u % 2)][:], ACT.Identity,
                              bias=cols[:, 0, bcol:bcol + 1]).then_inc(mlp["a_set"], 1)
                s_.activation(tanh_buf(u), bank[2 * (u % 2)][:], ACT.Tanh, scale=0.5,
                              bias=half_b1[:, k:k + 1]).then_inc(mlp["tanh_set"], 1)
            for c in range(NX):
                act.wait_ge(mlp["y_part"], 4 * (c + 1))
                bcol = COL["L0_xcond_b_m2"]
                s_.activation(xc_buf(c), bank[4 + c][:], ACT.Identity, scale=0.5,
                              bias=cols[:, 0, bcol:bcol + 1]).then_inc(mlp["y_set"], 1)

            norm("last")
            fulls(*LAST_Q)
            s = lp["last"]

            def body_last(n, p, first, last):
                t, j = 4 * n + 2 * p, 2 * p
                if not first:
                    for i in (0, 1):
                        halves(s, t - 4 + i, j + i, not (type(n) is int and n == 1))
                if not last:
                    for i in (0, 1):
                        act.wait_ge(s["nm"], t + i + 1)
                        if not first:
                            act.wait_ge(s["p_T"], t + i - 3)
                        s_.activation(e_buf(j + i), bank[j + i][:], ACT.Exp, scale=SCALE,
                                      bias=nmax[:, j + i, 0:1]).then_inc(s["expd"], 1)

            run(N, body_last)
            for i in (0, 1):
                halves(s, 4 * N - 2 + i, 2 + i, True)
            finish("last")
            act.wait_ge(out_T, 1)
            s_.activation(tok[:, 0:4, :].rearrange("p t f -> p (t f)"), bank[0][:], ACT.Copy).then_inc(out_set[0], 1)

        @block.vector
        def _(dve):
            v = nc.vector
            dve.wait_ge(vec_in, 16 * (len(VECTORS) + 1))
            v.tensor_copy(vecs_p[:].rearrange("r (d h) -> r d h", h=H),
                          vecs[:].rearrange("r (h d) -> r d h", h=H)).then_inc(vecs_set, 1)
            dve.wait_ge(cols_T, 1)
            v.tensor_copy(cols[:].rearrange("p a n -> p (a n)"), bank[7][:, 0:2 * NVEC]).then_inc(cols_set, 1)
            dve.wait_ge(cols_set, 1)
            v.tensor_scalar(half_b1[:], cols[:, 0, COL["L0_xcond_b_m1"]:COL["L0_xcond_b_m1"] + 4], 0.5, None,
                            ALU.mult).then_inc(cols_set, 1)
            dve.wait_ge(silu_exp, 1)
            v.tensor_scalar(silu_e[:], silu_e[:], 1.0, None, ALU.add).then_inc(cond_step, 1)
            dve.wait_ge(cond_step, 1)
            v.reciprocal(silu_e[:], silu_e[:]).then_inc(cond_step, 1)
            dve.wait_ge(cond_step, 2)
            v.tensor_tensor(silu_c[:], cols[:, 0, COND_AT:NVEC], silu_e[:], ALU.mult).then_inc(silu_set, 1)
            dve.wait_ge(mods_mm, 1)
            v.tensor_tensor(mods[:], bank[6][:, 0:NMOD * B].rearrange("p (m b) -> p m b", b=B),
                            cols[:, 0, 0:NMOD].unsqueeze(2).broadcast_to([P, NMOD, B]), ALU.add).then_inc(mods_set, 1)
            dve.wait_ge(mods_set, 1)
            scales = mods[:, 1:13, :].rearrange("p (m r) b -> p m r b", r=3)[:, 0:3, 0, :]
            v.tensor_scalar(scales, scales, 1.0, None, ALU.add).then_inc(cond_step, 1)
            scales = mods[:, 9:13, :].rearrange("p (m r) b -> p m r b", r=2)[:, :, 0, :]
            v.tensor_scalar(scales, scales, 1.0, None, ALU.add).then_inc(cond_step, 1)
            dve.wait_ge(cond_step, 4)
            dve.sem_inc(mods_set, 1)
            dve.wait_ge(x_T, 2)
            v.tensor_copy(chunk(xT, 1), bank[1][:]).then_inc(xT_set, 1)

            def norm(stage):
                s = ln
                at = LN_AT[stage]
                src, dst, chunks, eps, sc, sh, per = LN_OF[stage]
                for c0 in range(0, chunks, 2):
                    for c in (c0, c0 + 1):
                        dve.wait_ge(s["mean_mm"], at + c + 1)
                        if c >= 2:
                            dve.wait_ge(s["modulated"], MODULATED_AT[stage] + per * (c - 1))
                        elif stage != "self":
                            dve.wait_ge(s["modulated"], MODULATED_AT[stage])
                            dve.wait_ge(vals["set"], 6 if stage in ("mlp", "last") else 2)
                        v.tensor_tensor(xc_buf(c), chunk(src, c), bank[2 * (c % 2)][:],
                                        ALU.subtract).then_inc(s["centred"], 1)
                    for c in (c0, c0 + 1):
                        dve.wait_ge(s["rstd"], at + c + 1)
                        v.tensor_tensor(xc_buf(c), xc_buf(c), sq_buf(c), ALU.mult).then_inc(s["normed"], 1)

            def first_parts(first, end):
                for n0 in range(first, end, 2):
                    pair = n0 // 2
                    if pair in BUFFER_AFTER:
                        dve.wait_ge(stacked[BUFFER_AFTER[pair]], 16 * len(Q_PART))
                    for n in (n0, n0 + 1):
                        dve.wait_ge(split["full"], n + 1)
                        v.tensor_copy(part_buf(n, 0), full_buf(n)).then_inc(split["part0"], 1)
                    for n in (n0, n0 + 1):
                        dve.wait_ge(split["part0"], n + 1)
                        if n >= 2:
                            dve.wait_ge(split["part2"], n - 1)
                        v.tensor_tensor(rest_buf(n), full_buf(n), part_buf(n, 0), ALU.subtract).then_inc(
                            split["rest"], 1)
                    for n in (n0, n0 + 1):
                        dve.wait_ge(split["rest"], n + 1)
                        v.tensor_copy(part_buf(n, 1), rest_buf(n)).then_inc(split["part1"], 1)

            def middle_v_parts(stage):
                _, _, g0, groups = VALUES[stage]
                for i in range(groups):
                    rest = xc_buf(i).rearrange("p (t h d) -> p t h d", t=4, h=H)
                    m = v_number(g0, i)
                    dve.wait_ge(vals["part0"], m + 1)
                    if stage == "self" and i == 0:
                        dve.wait_ge(ln["modulated"], MODULATED_AT["self"] + B)
                        dve.wait_ge(ones_set, 5)
                    if i >= 2:
                        dve.wait_ge(vals["set"], m - 1)
                    v.tensor_tensor(rest, v_bank(g0 + i)[:].rearrange("p (t h d) -> p t h d", t=4, h=H),
                                    v_dst(stage, i, 0), ALU.subtract).then_inc(v_read, 1)
                    dve.wait_ge(v_read, g0 + i + 1)
                    v.tensor_copy(v_dst(stage, i, 1), rest).then_inc(vals["rest"], 1)

            def finish(stage):
                s = fin
                w, bcol, vcol, g = OUT[stage]
                dve.wait_ge(lp[stage]["o_set"], NT if stage == "self" else P // 4)
                v.reciprocal(rden[:], o_raw[:, :, :, D]).then_inc(s["recip"], 1)
                dve.wait_ge(s["recip"], FIN_AT[stage] + 1)
                for c in range(NX):
                    t = slice(4 * c, 4 * c + 4)
                    v.tensor_tensor(tok[:, t, :].rearrange("p t (h d) -> p h t d", h=H), o_raw[:, :, t, 0:D],
                                    rden[:, :, t].unsqueeze(3).broadcast_to([P, H, 4, D]),
                                    ALU.mult).then_inc(s["o_norm"], 1)
                for c in range(NX):
                    dve.wait_ge(s["y_set"], NX * FIN_AT[stage] + c + 1)
                    if g is None:
                        v.tensor_tensor(chunk(xT, c), chunk(xT, c), xc_buf(c), ALU.add).then_inc(s["x_new"], 1)
                    else:
                        for i in range(2):
                            b = 2 * c + i
                            xb = xT[:, b * L:(b + 1) * L]
                            last = v.scalar_tensor_tensor(xb, xc_buf(c)[:, i * L:(i + 1) * L], mods[:, g, b:b + 1], xb,
                                                          ALU.mult, ALU.add)
                        last.then_inc(s["x_new"], 1)

            norm("self")
            first_parts(*SELF_QK)
            middle_v_parts("self")
            for c in (1, 3):
                dve.wait_ge(ctx_T, c + 1)
                v.tensor_copy(chunk(ctxT, c), bank[c][:]).then_inc(ctxT_set, 1)
            first_parts(*CROSS_K)
            for i in range(B):
                g0 = VALUES["cross"][2]
                dve.wait_ge(vals["mm"], g0 + i + 1)
                last = v.tensor_copy(v_ctx[:, :, i, :, 0:D].rearrange("p h c e -> p c h e"),
                                     v_bank(g0 + i)[:].rearrange("p (t h d) -> p t h d", t=4, h=H)).then_inc(v_read, 1)
            dve.wait_ge(v_read, 2 + B)
            dve.sem_inc(v_copied, B)
            norm("ctx")

            s = lp["self"]

            def maxima_self(t, j0, first):
                for i in (0, 1):
                    j = j0 + i
                    dve.wait_ge(s["scores"], t + i + 1)
                    v.tensor_reduce(nmax[:, j, :], bank[j][:].rearrange("p (h k) -> p h k", h=4), AX_X,
                                    ALU.max).then_inc(s["topped"], 1)
                for i in (0, 1):
                    j = j0 + i
                    dve.wait_ge(s["topped"], t + i + 1)
                    if not first:
                        dve.wait_ge(s["p_T"], t + i - 3)
                    v.tensor_tensor(e_buf(j).rearrange("p (h k) -> p h k", h=4),
                                    bank[j][:].rearrange("p (h k) -> p h k", h=4),
                                    nmax[:, j, :].unsqueeze(2).broadcast_to([P, 4, P]),
                                    ALU.subtract).then_inc(s["scanned"], 1)

            def attend(s, N, maxima, sums):
                def body(n, p, first, last):
                    t, j = 4 * n + 2 * p, 2 * p
                    if not first:
                        for i in (0, 1):
                            rests(s, t - 4 + i, j + i)
                    if p == 0:
                        if not first and not (type(n) is int and n == 1):
                            sums(n - 2)
                        maxima(t + 2, 2, first)
                    elif not last:
                        maxima(t + 2, 0, False)

                maxima(0, 0, True)
                for n0 in (0, 1):
                    for p in (0, 1):
                        body(n0, p, n0 == 0, False)
                with dve.Fori(2, N - 1) as n:
                    for p in (0, 1):
                        body(n, p, False, False)
                for p in (0, 1):
                    body(N - 1, p, False, True)
                for i in (0, 1):
                    rests(s, 4 * N - 4 + i, i)
                sums(N - 2)
                for i in (0, 1):
                    rests(s, 4 * N - 2 + i, 2 + i)
                sums(N - 1)

            def run(N, body):
                for n0 in (0, 1):
                    for p in (0, 1):
                        body(n0, p, n0 == 0, False)
                with dve.Fori(2, N) as n:
                    for p in (0, 1):
                        body(n, p, False, False)

            def rests(s, t, j):
                dve.wait_ge(s["pT_set"], t + 1)
                v.scalar_tensor_tensor(pT_part(j, 1), bank[4 + j % 2][:], W_UP, pT_part(j, 0), ALU.mult,
                                       ALU.subtract).then_inc(s["rest_set"], 1)

            def sums_self(n):
                dve.wait_ge(s["pv"], 4 * n + 4)
                v.tensor_reduce(o_raw[:, :, bass.ds(n, 1), :].rearrange("p h t e -> p (h t) e"),
                                bank[O_BANK][:, 0:H * VP].rearrange("p (h s e) -> p h e s", h=H, s=3), AX_X,
                                ALU.add).then_inc(s["o_set"], 1)

            def sums_last(n):
                dve.wait_ge(s["pv"], 4 * n + 4)
                dst = o_raw[:].rearrange("p h t e -> p (h t e)")[:, bass.ds(n * (4 * DV), 4 * DV)]
                v.tensor_reduce(dst.rearrange("p (t e) -> p t e", t=4),
                                bank[O_BANK][:, 0:4 * VP].rearrange("p (t s e) -> p t e s", t=4, s=3), AX_X,
                                ALU.add).then_inc(s["o_set"], 1)

            attend(s, NT, maxima_self, sums_self)
            finish("self")
            norm("cross")
            first_parts(*CROSS_Q)

            s = lp["cross"]

            def body_cross(n, p, first, last):
                t, j0 = 4 * n + 2 * p, 2 * p
                for i in (0, 1):
                    j = j0 + i
                    dve.wait_ge(s["scores"], t + i + 1)
                    dve.sem_inc(turn, 1)
                    v.max(top[:, j, 0:8], bank[j][:]).then_inc(s["topped"], 1)
                for i in (0, 1):
                    j = j0 + i
                    dve.wait_ge(s["topped"], t + i + 1)
                    dve.sem_inc(turn, 1)
                    v.match_replace(s1_buf(j), top[:, j, 0:8], bank[j][:], TAKEN).then_inc(s["scanned"], 1)
                for i in (0, 1):
                    j = j0 + i
                    dve.wait_ge(s["scanned"], t + i + 1)
                    dve.sem_inc(turn, 1)
                    v.max(top[:, j, 8:16], s1_buf(j)).then_inc(chain, 1)
                for i in (0, 1):
                    j = j0 + i
                    dve.wait_ge(chain, t + i + 1)
                    if not first:
                        dve.wait_ge(s["p_ready"], t + i - 3)
                    dve.sem_inc(turn, 1)
                    v.match_replace(s2_buf(j), top[:, j, 8:16], s1_buf(j), TAKEN).then_inc(s["marked"], 1)

            run(P // 4, body_cross)
            first_parts(*LAST_K)
            middle_v_parts("last")
            finish("cross")

            norm("mlp")
            for u in range(2 * 4):
                c, k = divmod(u, 4)
                bcol = COL["L0_xcond_b_m1"] + 4 + k
                dve.wait_ge(mlp["tanh_set"], u + 1)
                v.scalar_tensor_tensor(full_buf(u), tanh_buf(u), 1.0, full_buf(u), ALU.add,
                                       ALU.mult).then_inc(mlp["gated"], 1)
                dve.wait_ge(mlp["gated"], u + 1)
                dve.wait_ge(mlp["b_mm"], u + 1)
                if u >= 2:
                    dve.wait_ge(mlp["y_part"], u - 1)
                v.scalar_tensor_tensor(sq_buf(u), bank[2 * (u % 2) + 1][:], cols[:, 0, bcol:bcol + 1], full_buf(u),
                                       ALU.add, ALU.mult).then_inc(mlp["hidden"], 1)
            for c in range(NX):
                dve.wait_ge(mlp["y_set"], c + 1)
                for i in range(2):
                    b = 2 * c + i
                    xb = xT[:, b * L:(b + 1) * L]
                    last = v.scalar_tensor_tensor(xb, xc_buf(c)[:, i * L:(i + 1) * L], mods[:, G_MLP, b:b + 1], xb,
                                                  ALU.mult, ALU.add)
                last.then_inc(mlp["x_new"], 1)

            norm("last")
            first_parts(*LAST_Q)
            s = lp["last"]

            def maxima_last(t, j0, first):
                for i in (0, 1):
                    dve.wait_ge(s["scores"], t + i + 1)
                    if not first:
                        dve.wait_ge(s["expd"], t + i - 3)
                    v.tensor_reduce(top[:, j0 + i, 0:1], bank[j0 + i][:], AX_X, ALU.max).then_inc(s["topped"], 1)

            attend(s, P // 4, maxima_last, sums_last)
            finish("last")
            dve.wait_ge(out_T, 2)
            v.tensor_copy(tok[:, 4:8, :].rearrange("p t f -> p (t f)"), bank[1][:]).then_inc(out_set[1], 1)

        @block.tensor
        def _(pe):
            t_ = nc.tensor
            mm = t_.matmul
            pe.wait_ge(ident_set, 2)
            pe.wait_ge(vec_in, 16 * (len(VECTORS) + 1))
            pe.wait_ge(vecs_set, 1)
            t_.transpose(bank[7][:, 0:NVEC], vecs[:], ident[0:NVEC, 0:NVEC])
            t_.transpose(bank[7][:, NVEC:2 * NVEC], vecs_p[:],
                         ident[0:NVEC, 0:NVEC]).then_inc(cols_T, 1)
            pe.wait_ge(x_in, 48)
            for t in range(NT):
                last = t_.transpose(bank[t // 4][:, (t % 4) * P:(t % 4 + 1) * P], tok[:, t, :], ident[:])
                if t % 4 == 3:
                    last.then_inc(x_T, 1)
            pe.wait_ge(ada_in, 48)
            pe.wait_ge(silu_set, 1)
            for m in range(NMOD):
                w = w_ada[:, m * C:(m + 1) * C] if m < 9 else w_ss[:, (m - 9) * C:(m - 8) * C]
                last = mm(bank[6][:, m * B:(m + 1) * B], w, silu_c[:], start=True, stop=True)
            last.then_inc(mods_mm, 1)
            pe.wait_ge(ones_set, 2)
            pe.wait_ge(xT_set, 2)

            def norm(stage):
                s = ln
                at = LN_AT[stage]
                src, dst, chunks, eps, sc, sh, per = LN_OF[stage]
                if stage in x_before:
                    pe.wait_ge(*x_before[stage])
                for c0 in range(0, chunks, 2):
                    for c in (c0, c0 + 1):
                        if c >= 2:
                            pe.wait_ge(s["centred"], at + c - 1)
                        mm(bank[2 * (c % 2)][:], mean_w[:], chunk(src, c), start=True,
                           stop=True).then_inc(s["mean_mm"], 1)
                    for c in (c0, c0 + 1):
                        pe.wait_ge(s["squared"], at + c + 1)
                        mm(bank[2 * (c % 2) + 1][:], mean_w[:], sq_buf(c), start=True,
                           stop=True).then_inc(s["var_mm"], 1)

            def project(first, end):
                for n in range(first, end):
                    w, _, src, c = UNITS[n]
                    if n in (SELF_QK[0], SELF_QK[0] + 1):
                        pe.wait_ge(ln["modulated"], MODULATED_AT["self"] + 2 * (c + 1))
                    elif n >= CROSS_Q[0] and src is hT:
                        pe.wait_ge(ln["modulated"], MODULATED_AT["cross" if n < LAST_K[0] else "last"] + 2 * (c + 1))
                    if n >= 2:
                        pe.wait_ge(split["full"], n - 1)
                    mm(unit_bank(n)[:], w, chunk(src, c), start=True, stop=True).then_inc(split["full_mm"], 1)

            def values(stage):
                w, src, g0, groups = VALUES[stage]
                for i in range(groups):
                    if g0 + i >= 2:
                        pe.wait_ge(v_read, g0 + i - 1)
                    for k in range(4):
                        t = 4 * i + k
                        last = mm(v_bank(g0 + i)[:, k * C:(k + 1) * C], src[:, t * P:(t + 1) * P], w, start=True,
                                  stop=True)
                    last.then_inc(vals["mm"], 1)

            def left(s, n, j, more):
                name = "pT_set" if s is lp["cross"] else "rest_set"
                pe.wait_ge(s[name], 4 * n + j + (1 if more else -1))

            def transposes(s, n, j, ready, first):
                pe.wait_ge(s[ready], 4 * n + j + 1)
                if not (first and j < 2):
                    left(s, n, j, 0)
                for i in range(4):
                    last = t_.transpose(bank[4 + j % 2][:, i * P:(i + 1) * P], e_buf(j)[:, i * P:(i + 1) * P], ident[:])
                last.then_inc(s["p_T"], 1)

            def finish(stage):
                s = fin
                w, bcol, vcol, g = OUT[stage]
                for c in range(NX):
                    pe.wait_ge(s["o_norm"], NX * FIN_AT[stage] + c + 1)
                    for i in range(4):
                        last = t_.transpose(bank[2 * c][:, i * P:(i + 1) * P], tok[:, 4 * c + i, :], ident[:])
                    last.then_inc(s["o_T"], 1)
                for c in range(NX):
                    pe.wait_ge(s["oT_set"], NX * FIN_AT[stage] + c + 1)
                    mm(bank[2 * c + 1][:], w, chunk(hT, c), start=True, stop=True).then_inc(s["y_mm"], 1)

            def wait_stacked(*pairs):
                for pair in pairs:
                    pe.wait_ge(stacked[pair], 16 * len(Q_PART))

            norm("self")
            pe.wait_ge(w_in, 160)
            pe.wait_ge(w_qk_set, 6)
            project(*SELF_QK)
            values("self")
            pe.wait_ge(ctx_in, 16)
            for t in range(NCT):
                last = t_.transpose(bank[t // 4][:, (t % 4) * P:(t % 4 + 1) * P], ctx_tok[:, t, :], ident[:])
                if t % 4 == 3:
                    last.then_inc(ctx_T, 1)
            pe.wait_ge(ctxT_set, 4)
            project(*CROSS_K)
            values("cross")
            norm("ctx")
            pe.wait_ge(ln["modulated"], MODULATED_AT["ctx"] + B)
            pe.wait_ge(split["full"], CROSS_K[1])
            pe.wait_ge(vals["set"], 2)
            pe.wait_ge(v_copied, B)
            pe.wait_ge(win_in, 32)
            wait_stacked(0, 1)

            s = lp["self"]

            def scores_self(n, j, first):
                t = 4 * n + j
                if not first:
                    pe.wait_ge(s["scanned"], t - 3)
                for i in range(4):
                    at = n * P + (4 * j + i) * NTOK
                    last = mm(bank[j][:, i * P:(i + 1) * P], q_stack[:, bass.ds(at, P)], k_stack[:, bass.ds(at, P)],
                              start=True, stop=True)
                last.then_inc(s["scores"], 1)

            def pv_self(n, p, first):
                for j in (2 * p, 2 * p + 1):
                    left(s, n, j, 1)
                    pe.wait_ge(s["staged"], 4 * n + j + 1)
                    if j == 0 and not first:
                        pe.wait_ge(s["o_set"], n)
                    for i in range(4):
                        h = 4 * j + i
                        for part in (0, 1):
                            last = mm(bank[O_BANK][:, h * VP:(h + 1) * VP], pT_part(j, part)[:, i * P:(i + 1) * P],
                                      v_stage3[:, j, i * VP:(i + 1) * VP], start=(part == 0), stop=(part == 1))
                    last.then_inc(s["pv"], 1)

            def attend(s, N, scores, pv, ready, back=None):
                def body(n, p, first, last):
                    for i in (0, 1):
                        if p == 0:
                            scores(n, 2 + i, first)
                        elif not last:
                            scores(n + 1, i, False)
                    if back and p == 1 and not first and not (type(n) is int and n == 1):
                        back(n - 2)
                    for i in (0, 1):
                        if p == 1:
                            transposes(s, n, i, ready, first)
                        elif not first:
                            transposes(s, n - 1, 2 + i, ready, type(n) is int and n == 1)
                    if not first:
                        pv(n - 1, p, type(n) is int and n == 1)

                scores(0, 0, True)
                scores(0, 1, True)
                for n0 in (0, 1):
                    for p in (0, 1):
                        body(n0, p, n0 == 0, False)
                with pe.Fori(2, N - 1) as n:
                    for p in (0, 1):
                        body(n, p, False, False)
                for p in (0, 1):
                    body(N - 1, p, False, True)
                if back:
                    back(N - 2)
                for i in (0, 1):
                    transposes(s, N - 1, 2 + i, ready, False)
                for p in (0, 1):
                    pv(N - 1, p, False)
                if back:
                    back(N - 1)

            attend(s, NT, scores_self, pv_self, "expd")
            finish("self")
            norm("cross")
            project(*CROSS_Q)
            wait_stacked(2, 3, 4)

            def scores_ctx(s, frees):
                def f(n, j, first):
                    t = 4 * n + j
                    if not first:
                        for name in frees:
                            pe.wait_ge(s[name], t - 3)
                    g = 2 * n + j // 2
                    mm(bank[j][:], q_stack[0:KS, bass.ds(g * L + (j % 2) * P, P)], k_stack[0:KS, bass.ds(g * LC, LC)],
                       start=True, stop=True).then_inc(s["scores"], 1)
                return f

            def pv_cross(n, p, first):
                s = lp["cross"]
                left(s, n, 2 * p + 1, 1)
                pe.wait_ge(s["staged"], 2 * n + p + 1)
                if p == 0 and not first:
                    pe.wait_ge(s["o9_set"], n)
                for c in range(KC):
                    last = mm(bank[O_BANK][0:DV, 2 * p * P:2 * (p + 1) * P], v_stage[:, 2 * p, c * DV:(c + 1) * DV],
                              pT_pair[:, 2 * p:2 * p + 2, c * P:(c + 1) * P], start=(c == 0), stop=(c == KC - 1))
                last.then_inc(s["pv"], 2)

            def back_cross(n):
                s = lp["cross"]
                pe.wait_ge(s["o9_set"], n + 1)
                pe.sem_inc(pe_turn, 1)
                for j in range(4):
                    last = t_.transpose(bank[BACK_BANK][:, j * DV:(j + 1) * DV], o9[:, j * P:(j + 1) * P],
                                        ident[0:DV, 0:DV])
                last.then_inc(s["back_T"], 1)

            def pv_last(n, p, first):
                s = lp["last"]
                for j in (2 * p, 2 * p + 1):
                    left(s, n, j, 1)
                    pe.wait_ge(s["staged"], 2 * n + p + 1)
                    if j == 0 and not first:
                        pe.wait_ge(s["o_set"], n)
                    for c in range(KC):
                        for part in (0, 1):
                            last = mm(bank[O_BANK][:, j * VP:(j + 1) * VP], pT_part(j, part)[:, c * P:(c + 1) * P],
                                      v_stage3[:, 2 * p, c * VP:(c + 1) * VP], start=(c == 0 and part == 0),
                                      stop=(c == KC - 1 and part == 1))
                    last.then_inc(s["pv"], 1)

            s = lp["cross"]
            attend(s, P // 4, scores_ctx(s, ("expd",)), pv_cross, "p_ready", back_cross)
            pe.wait_ge(s["o_set"], P // 4)
            project(*LAST_K)
            values("last")
            finish("cross")

            norm("mlp")
            pe.wait_ge(ln["modulated"], MODULATED_AT["mlp"] + 4)

            def down(u):
                c, k = divmod(u, 4)
                pe.wait_ge(mlp["hidden"], u + 1)
                last = mm(bank[4 + c][:], w_m2[:, k, :], sq_buf(u), start=(k == 0), stop=(k == 3))
                last.then_inc(mlp["y_part"], 1)

            for u in range(2 * 4):
                c, k = divmod(u, 4)
                if u >= 2:
                    pe.wait_ge(mlp["tanh_set"], u - 1)
                mm(bank[2 * (u % 2)][:], w_m1[:, k * P:(k + 1) * P], chunk(hT, c), start=True,
                   stop=True).then_inc(mlp["a_mm"], 1)
                if u >= 2:
                    down(u - 2)
                mm(bank[2 * (u % 2) + 1][:], w_m1[:, HID + k * P:HID + (k + 1) * P], chunk(hT, c), start=True,
                   stop=True).then_inc(mlp["b_mm"], 1)
            down(6)
            down(7)

            norm("last")
            project(*LAST_Q)
            pe.wait_ge(vals["set"], 2 + B)
            wait_stacked(5, 6, 7)
            s = lp["last"]
            attend(s, P // 4, scores_ctx(s, ("expd",)), pv_last, "expd")
            finish("last")
            for c in range(NX):
                pe.wait_ge(fin["x_new"], 2 * NX + c + 1)
                for i in range(4):
                    t = 4 * c + i
                    last = t_.transpose(bank[c][:, i * P:(i + 1) * P], xT[:, t * P:(t + 1) * P], ident[:])
                last.then_inc(out_T, 1)


_OUT_SHAPE = (B, L, C)


def kernel(**inputs):
    import numpy as _np
    import concourse.bacc as _bacc
    from concourse.bass_utils import run_bass_kernel_spmd as _run

    nc = _bacc.Bacc("TRN2", target_bir_lowering=False, num_devices=1)
    arrays, args = {}, {}
    for name, value in inputs.items():
        value = _np.ascontiguousarray(value)
        arrays[f"in_{name}"] = value
        args[name] = nc.dram_tensor(f"in_{name}", value.shape, mybir.dt.from_np(value.dtype), kind="ExternalInput").ap()
    out = nc.dram_tensor("out", _OUT_SHAPE, F32, kind="ExternalOutput").ap()
    pixart_kernel(nc, args, out)
    r = _run(nc, [arrays], core_ids=[0])
    return r.results[0]["out"]
```

```python
from contextlib import ExitStack

import concourse.bass as bass
from concourse import mybir

F32 = mybir.dt.float32
BF16 = mybir.dt.bfloat16
F16 = mybir.dt.float16
ALU = mybir.AluOpType
ACT = mybir.ActivationFunctionType
AX_X = mybir.AxisListType.X

P = 128
B, L, LC, C = 4, 256, 512, 128
H = 16
D = C // H
HID = 512
WIN, SHIFT = 64, 32
EPS0, EPS1 = 1e-6, 1e-5
SCALE = float(D) ** -0.5
LN_EXP_SET, TANH_SET = 6, 0
TAKEN = -3.0e38

NTOK = B * L
NCTX = B * LC
NT = NTOK // P
NCT = NCTX // P
CH = 512
NX = NTOK // CH
KC = LC // P
DV = D + 1

Q_PART = (0, 0, 0, 1, 1, 2)
K_PART = (0, 1, 2, 0, 1, 0)
KS = D * len(Q_PART)
SECOND = KS
KW = SECOND + KS
W_UP = 4096.0
VP = 3 * DV

VECTORS = (
    ("L0_xcond_b_ada", 9), ("L1_xcond_bss_q", 2), ("L1_xcond_bss_kv", 2), ("L0_xcond_b_qkv", 3),
    ("L0_xcond_b_so", 1), ("L0_xcond_b_q", 1), ("L0_xcond_b_kv", 2), ("L0_xcond_b_co", 1),
    ("L0_xcond_b_m1", 8), ("L0_xcond_b_m2", 1), ("L1_xcond_bq", 1), ("L1_xcond_bkv", 2),
    ("L1_xcond_bp", 1),
)
COL = {}
_at = 0
for _name, _rows in VECTORS:
    COL[_name] = _at
    _at += _rows
COND_AT = _at
NVEC = _at + B
NMOD = 13
SH_MSA, SC_MSA, G_MSA, SH_MCA, SC_MCA, G_MCA, SH_MLP, SC_MLP, G_MLP, SC_Q, SH_Q, SC_KV, SH_KV = range(NMOD)


def pixart_kernel(nc, a, out):
    def load_tables(act, table_set):
        act.add_instruction(mybir.InstLoadActFuncSet(name=nc.get_next_instruction_name(),
                                                     act_func_set_id=table_set, ins=[], outs=[]))

    with ExitStack() as ctx:
        def sb(name, shape, dt=F32):
            return ctx.enter_context(nc.sbuf_tensor(name, shape, dt))

        def sem(name):
            return ctx.enter_context(nc.semaphore(name))

        ident = sb("ident", [P, P])
        mean_w = sb("mean_w", [P, P])
        neg_scale = sb("neg_scale", [P, 1])
        vecs = sb("vecs", [NVEC, P])
        vecs_p = sb("vecs_p", [NVEC, P])
        w_qk = sb("w_qk", [P, 6, C])
        cols = sb("cols", [P, 2, NVEC])
        half_b1 = sb("half_b1", [P, 4])
        w_qkv = sb("w_qkv", [P, 3 * C])
        w_so = sb("w_so", [P, C])
        w_q = sb("w_q", [P, C])
        w_kv = sb("w_kv", [P, 2 * C])
        w_co = sb("w_co", [P, C])
        w_m1 = sb("w_m1", [P, 2 * HID])
        w_m2 = sb("w_m2", [P, HID // P, C])
        w1_q = sb("w1_q", [P, C])
        w1_kv = sb("w1_kv", [P, 2 * C])
        w1_p = sb("w1_p", [P, C])
        silu_c = sb("silu_c", [P, B])
        silu_e = sb("silu_e", [P, B])
        mods = sb("mods", [P, NMOD, B])
        tok = sb("tok", [P, NT, P])
        xT = sb("xT", [P, NTOK])
        ctxT = sb("ctxT", [P, NCTX])
        q_stack = sb("q_stack", [KW, H * NTOK], BF16)
        k_all = sb("k_all", [P, H * NCTX], BF16)
        k_stack = k_all[0:KS, :]
        k_windows = k_all[:, 0:H * NT * WIN]
        k_late = k_all[:, H * NTOK:].bitcast(F32)
        ctx_tok = k_late[:, 0:NCTX].rearrange("p (t f) -> p t f", f=P)
        w_ada = k_late[:, NCTX:NCTX + 9 * C]
        w_ss = k_late[:, NCTX + 9 * C:NCTX + 13 * C]
        v_self = sb("v_self", [P, NT, H, VP], BF16)
        v_all = sb("v_all", [P, H * B * KC * VP], BF16)
        v_ctx = v_all[:, 0:2 * H * B * KC * DV].bitcast(F32).rearrange("p (h b c e) -> p h b c e", h=H, b=B, c=KC)
        v_last = v_all[:].rearrange("p (h b c e) -> p h b c e", h=H, b=B, c=KC)
        o_raw = sb("o_raw", [P, H, NT, DV])
        o_flat = o_raw[:].rearrange("p h t e -> p (h t e)")
        rden = sb("rden", [P, H, NT])
        o9 = sb("o9", [DV, CH])
        top = sb("top", [P, 4, 16])
        nmax = sb("nmax", [P, 4, 8])
        parts_own = sb("parts_own", [P, 2, 3, 2 * CH], BF16)
        work = sb("work", [P, 14, CH])
        v_stage = sb("v_stage", [P, 4, KC * DV])
        v_stage3 = sb("v_stage3", [P, 4, 4 * VP], BF16)
        v_pairs = sb("v_pairs", [P, 2, 2 * (H // 2), 2, VP], BF16)

        def e_buf(j):
            return work[:, j, :]

        pT_pair = work[:, 4:8, :]

        def pT_buf(j):
            return work[:, 4 + j, :]

        def pT_part(j, i):
            return pT_buf(j).bitcast(F16)[:, i * CH:(i + 1) * CH]

        def s2_buf(j):
            return work[:, 8 + j, :]

        def s1_buf(j):
            return work[:, 12 + j % 2, :]

        def xc_buf(c):
            return work[:, c % 2, :]

        def sq_buf(c):
            return work[:, 2 + c % 2, :]

        def xc_of(stage, c):
            return parts_own[:, 1].rearrange("p s n -> p (s n)").bitcast(F32)[:, c * CH:(c + 1) * CH] \
                if stage == "ctx_b" else xc_buf(c)

        def sq_of(stage, c):
            return parts_own[:, 0].rearrange("p s n -> p (s n)").bitcast(F32)[:, c * CH:(c + 1) * CH] \
                if stage == "ctx_b" else sq_buf(c)

        def mean_bank(stage, c):
            return bank[4 + c] if stage == "ctx_b" else bank[2 * c]

        def var_bank(stage, c):
            return bank[6 + c] if stage == "ctx_b" else bank[2 * c + 1]

        hT = work[:, 4:6, :].rearrange("p c n -> p (c n)")

        def rest_buf(i):
            return work[:, 6 + i % 2, :]

        def full_buf(u):
            return work[:, 10 + u % 2, :]

        def v_rest_buf(stage, i):
            return work[:, 12 + i % 2, :] if stage == "last" else o_flat[:, (i % 2) * CH:(i % 2 + 1) * CH]

        def tanh_buf(u):
            return work[:, 8 + u % 2, :]

        parts_work = work[:, 8:14, :].rearrange("p a n -> p (a n)").bitcast(BF16).rearrange(
            "p (r s n) -> p r s n", r=2, s=3)

        def pair_parts(pair):
            return parts_work[:, pair - 2] if pair in (2, 3) else parts_own[:, pair % 2]

        def part_buf(n, i):
            return pair_parts(n // 2)[:, i, (n % 2) * CH:(n % 2 + 1) * CH]

        BUFFER_AFTER = {4: 0, 5: 1, 6: 4, 7: 5}

        def stacked_by(pair):
            return 16 * len(Q_PART) * (2 if pair < 2 else 1)

        bank = [ctx.enter_context(nc.psum_tensor(f"bank{i}", [P, 512], F32)) for i in range(8)]
        O_BANK, BACK_BANK = 6, 7

        def unit_bank(n):
            return bank[4 + n % 2]

        def v_bank(g):
            return bank[6 + g % 2]

        ones_set = sem("ones_set")
        v_pairs_set = sem("v_pairs_set")
        ident_set = sem("ident_set")
        zeros_set = sem("zeros_set")
        vec_in = sem("vec_in")
        x_in = sem("x_in")
        ctx_in = sem("ctx_in")
        ada_in = sem("ada_in")
        w_in = sem("w_in")
        w_late_in = sem("w_late_in")
        cols_T = sem("cols_T")
        cols_set = sem("cols_set")
        vecs_set = sem("vecs_set")
        w_qk_set = sem("w_qk_set")
        cond_step = sem("cond_step")
        silu_exp = sem("silu_exp")
        silu_set = sem("silu_set")
        mods_mm = sem("mods_mm")
        mods_set = sem("mods_set")
        x_T = sem("x_T")
        xT_set = sem("xT_set")
        ctx_T = sem("ctx_T")
        ctxT_set = sem("ctxT_set")
        out_T = sem("out_T")
        out_set = [sem(f"out_set{c}") for c in range(NX)]
        stored = sem("stored")

        def stage_sems(names, stage):
            return {n: sem(f"{n}_{stage}") for n in names}

        ln = stage_sems(("mean_mm", "centred", "squared", "var_mm", "log_var", "rstd", "normed", "modulated", "modulated_v"), "norm")
        NORMS = ("self", "ctx_b", "cross", "ctx_a", "mlp", "last")
        LN_AT = {stage: 2 * i for i, stage in enumerate(NORMS)}
        MODULATED_AT = {stage: 2 * i for i, stage in enumerate(("self", "cross", "ctx_b", "ctx_a", "mlp", "last"))}
        MODULATED_V_BEFORE = {"self": 0, "cross": 1, "ctx_a": 2, "mlp": 2, "last": 3}
        split = stage_sems(("full_mm", "part0", "rest", "part1", "part2"), "split")
        stacked = [sem(f"stacked{i}") for i in range(8)]
        vals = stage_sems(("mm", "part0", "rest", "set"), "v")
        fin = stage_sems(("recip", "o_norm", "o_T", "oT_set", "y_mm", "y_set", "x_new"), "out")
        FIN_AT = {"self": 0, "cross": 1, "last": 2}
        lp = {
            "self": stage_sems(("scores", "topped", "scanned", "expd", "p_T", "pT_set", "rest_set", "pv", "o_set"), "self"),
            "cross": stage_sems(("scores", "topped", "nm", "scanned", "expd", "marked", "masked", "p_ready", "p_T",
                                 "pT_set", "pv", "o9_set", "back_T", "o_set"), "cross"),
            "last": stage_sems(("scores", "topped", "nm", "expd", "p_T", "pT_set", "rest_set", "pv", "o_set"), "last"),
        }
        for _s in lp:
            lp[_s]["staged"] = sem(f"staged_{_s}")
        chain = sem("chain")
        turn = sem("turn")
        pool_turn = sem("pool_turn")
        pe_turn = sem("pe_turn")
        mlp = stage_sems(("a_mm", "b_mm", "a_set", "tanh_set", "gated", "hidden", "y_part", "y_set", "x_new"), "mlp")

        x_before = {"self": (xT_set, 2), "cross": (fin["x_new"], NX), "mlp": (fin["x_new"], 2 * NX),
                    "last": (mlp["x_new"], NX)}
        LN_OF = {
            "self": (xT, hT, 0, EPS0, SC_MSA, SH_MSA, 2),
            "cross": (xT, hT, 0, EPS0, SC_MCA, SH_MCA, 2),
            "mlp": (xT, hT, 0, EPS0, SC_MLP, SH_MLP, 2),
            "last": (xT, hT, 0, EPS1, SC_Q, SH_Q, 2),
            "ctx_a": (ctxT, ctxT, 0, EPS1, SC_KV, SH_KV, 1),
            "ctx_b": (ctxT, ctxT, 2, EPS1, SC_KV, SH_KV, 1),
        }

        def chunk(t, c):
            return t[:, c * CH:(c + 1) * CH]

        bqkv, bkv, b1kv = COL["L0_xcond_b_qkv"], COL["L0_xcond_b_kv"], COL["L1_xcond_bkv"]
        UNITS = (
            [(w_qk[:, 0, :], bqkv, hT, c) for c in range(NX)]
            + [(w_qk[:, 1, :], bqkv + 1, hT, c) for c in range(NX)]
            + [(w_qk[:, 3, :], bkv, ctxT, c) for c in range(B)]
            + [(w_qk[:, 2, :], COL["L0_xcond_b_q"], hT, c) for c in range(NX)]
            + [(w_qk[:, 5, :], b1kv, ctxT, c) for c in range(B)]
            + [(w_qk[:, 4, :], COL["L1_xcond_bq"], hT, c) for c in range(NX)]
        )
        SELF_QK, CROSS_K, CROSS_Q, LAST_K, LAST_Q = (0, 4), (4, 8), (8, 10), (10, 14), (14, 16)
        VALUES = {
            "cross": (w_kv[:, C:2 * C], ctxT, 0, B),
            "self": (w_qkv[:, 2 * C:3 * C], hT, B, NT // 4),
            "last": (w1_kv[:, C:2 * C], ctxT, 6, B),
        }
        OUT = {
            "self": (w_so[:], COL["L0_xcond_b_so"], bqkv + 2, G_MSA),
            "cross": (w_co[:], COL["L0_xcond_b_co"], bkv + 1, G_MCA),
            "last": (w1_p[:], COL["L1_xcond_bp"], b1kv + 1, None),
        }

        v_copied = sem("v_copied")
        v_read = sem("v_read")

        def v_number(g0, i):
            return i + (0 if g0 == B else 2)

        def v_dst(stage, i, part):
            e = slice(part * DV, part * DV + D)
            if stage == "self":
                return v_self[:, 4 * i:4 * i + 4, :, e]
            return v_last[:, :, i, :, e].rearrange("p h c e -> p c h e")

        block = ctx.enter_context(nc.Block())

        LATE_WEIGHTS = ((w_so[:], "L0_xcond_w_so"), (w_q[:], "L0_xcond_w_q"), (w_co[:], "L0_xcond_w_co"),
                        (w1_q[:], "L1_xcond_Wq"), (w1_kv[:], "L1_xcond_Wkv"), (w1_p[:], "L1_xcond_Wp"),
                        (w_m1[:], "L0_xcond_w_m1"))
        N_LATE = len(LATE_WEIGHTS) + 1

        @block.sync
        def _(sp):
            x = a["x"]
            tiles = tok[:].rearrange("p (b h) f -> p b h f", h=2)
            sp.dma_start(tiles[:, :, 0, :], x[:, SHIFT:SHIFT + P, :].rearrange("b p f -> p b f")).then_inc(x_in, 16)
            sp.dma_start(tiles[0:P - SHIFT, :, 1, :],
                         x[:, SHIFT + P:L, :].rearrange("b p f -> p b f")).then_inc(x_in, 16)
            sp.dma_start(tiles[P - SHIFT:P, :, 1, :],
                         x[:, 0:SHIFT, :].rearrange("b p f -> p b f")).then_inc(x_in, 16)
            sp.dma_start(ctx_tok, a["ctx_1024"].rearrange("b (c p) f -> p (b c) f", p=P)).then_inc(ctx_in, 16)
            sp.dma_start(vecs[COND_AT:NVEC, :], a["cond_1024"]).then_inc(vec_in, 16)
            for name, rows in VECTORS:
                at = COL[name]
                sp.dma_start(vecs[at:at + rows, :], a[name].rearrange("(r n) -> r n", n=P)).then_inc(vec_in, 16)
            for dst, name in LATE_WEIGHTS:
                sp.dma_start(dst, a[name]).then_inc(w_late_in, 16)
            sp.dma_start(w_m2[:], a["L0_xcond_w_m2"].rearrange("(k p) n -> p k n", p=P)).then_inc(w_late_in, 16)
            def stack(pair, kind):
                parts = pair_parts(pair)
                if kind == "k":
                    k0 = UNITS[2 * pair][3]
                    dst = k_stack.rearrange("r (h b n) -> r h b n", h=H, b=B)[:, :, k0:k0 + 2, :].rearrange(
                        "r h b n -> r h (b n)")
                else:
                    dst = q_stack[:].rearrange("r (h n) -> r h n", h=H)
                for t, part in enumerate(Q_PART if kind == "q" else K_PART):
                    sp.wait_ge(split[f"part{part}"], 2 * pair + 2)
                    sp.dma_start(dst[D * t:D * t + D], parts[:, part, :]).then_inc(stacked[pair], 16)

            def stack_windows(pair, kind):
                parts = pair_parts(pair)
                q_dst = q_stack[:].rearrange("r (h t w n) -> r h t w n", h=H, w=2, n=WIN)
                k_dst = k_windows.rearrange("r (h t n) -> r h t n", h=H, n=WIN)
                for t, part in enumerate(Q_PART if kind == "q" else K_PART):
                    sp.wait_ge(split[f"part{part}"], 2 * pair + 2)
                    src = parts[:, part, :].rearrange("p (t w n) -> p t w n", w=2, n=WIN)
                    for w in (0, 1):
                        rows = slice(SECOND * w + D * t, SECOND * w + D * t + D)
                        dst = q_dst[rows, :, :, w, :] if kind == "q" else k_dst[rows]
                        sp.dma_start(dst, src[:, :, w, :]).then_inc(stacked[pair], 16)

            sp.wait_ge(zeros_set, 1)
            stack_windows(0, "q")
            stack_windows(1, "k")
            sp.wait_ge(lp["self"]["scores"], NT * 2)
            stack(2, "k")
            stack(3, "k")
            stack(4, "q")
            sp.wait_ge(lp["cross"]["scores"], P)
            stack(5, "k")
            stack(6, "k")
            stack(7, "q")
            for c in range(NX):
                sp.wait_ge(out_set[c], 1)
                rows = out[2 * c:2 * c + 2]
                done = tiles[:, 2 * c:2 * c + 2]
                sp.dma_start(rows[:, SHIFT:SHIFT + P, :].rearrange("b p f -> p b f"),
                             done[:, :, 0, :]).then_inc(stored, 16)
                sp.dma_start(rows[:, SHIFT + P:L, :].rearrange("b p f -> p b f"),
                             done[0:P - SHIFT, :, 1, :]).then_inc(stored, 16)
                sp.dma_start(rows[:, 0:SHIFT, :].rearrange("b p f -> p b f"),
                             done[P - SHIFT:P, :, 1, :]).then_inc(stored, 16)
            sp.wait_ge(stored, 16 * 3 * NX)

        @block.gpsimd
        def _(pool):
            g = nc.gpsimd
            g.memset(ident[:], 0.0).then_inc(ident_set, 1)
            g.memset(neg_scale[:], -SCALE).then_inc(ones_set, 1)
            g.memset(mean_w[:], 1.0 / C).then_inc(ones_set, 1)
            pool.wait_ge(ident_set, 1)
            g.affine_select(out=ident[:], in_=ident[:], compare_op=ALU.not_equal, fill=1.0, base=0,
                            pattern=[[-1, P]], channel_multiplier=1).then_inc(ident_set, 1)
            g.memset(v_self[:, :, :, D:VP], 0.0).then_inc(ones_set, 1)
            g.memset(v_pairs[:], 0.0).then_inc(v_pairs_set, 1)
            pool.dma_start(w_ada, a["L0_xcond_w_ada"]).then_inc(ada_in, 16)
            pool.dma_start(w_ss[:, 0:2 * C], a["L1_xcond_Wss_q"]).then_inc(ada_in, 16)
            pool.dma_start(w_ss[:, 2 * C:], a["L1_xcond_Wss_kv"]).then_inc(ada_in, 16)
            g.memset(v_ctx[:, :, :, :, D:DV], 1.0).then_inc(ones_set, 1)
            pool.wait_ge(ones_set, 4)
            g.memset(v_self[:, :, :, D:DV], 1.0).then_inc(ones_set, 1)
            for i, w in ((0, w_qkv[:, 0:C]), (1, w_qkv[:, C:2 * C]), (3, w_kv[:, 0:C]),
                               (2, w_q[:]), (5, w1_kv[:, 0:C]), (4, w1_q[:])):
                if i == 0:
                    pool.wait_ge(w_in, 32)
                if i == 2:
                    pool.wait_ge(w_late_in, 16 * N_LATE)
                g.tensor_copy(w_qk[:, i, :].rearrange("p (d h) -> p d h", h=H),
                              w.rearrange("p (h d) -> p d h", h=H)).then_inc(w_qk_set, 1)

            def last_parts(first, end):
                for n in range(first, end):
                    pool.wait_ge(split["part1"], n + 1)
                    g.tensor_tensor(part_buf(n, 2), rest_buf(n), part_buf(n, 1), ALU.subtract).then_inc(
                        split["part2"], 1)

            def last_v_parts(stage, first, end):
                g0 = VALUES[stage][2]
                for i in range(first, end):
                    pool.wait_ge(vals["rest"], v_number(g0, i) + 1)
                    g.tensor_tensor(v_dst(stage, i, 2), v_rest_buf(stage, i).rearrange("p (t h d) -> p t h d", t=4, h=H),
                                    v_dst(stage, i, 1), ALU.subtract).then_inc(vals["set"], 1)

            def stage_self(n, p, first):
                s = lp["self"]
                vf = v_self[:].rearrange("p t h e -> p (t h e)")
                if not first:
                    pool.wait_ge(s["pv"], 4 * n + 2 * p - 2)
                for par in (0, 1):
                    rows = slice(64 * par, 64 * par + 64)
                    pool.sem_inc(pool_turn, 1)
                    g.tensor_copy(v_pairs[rows, p, :, par, :],
                                  vf[rows, bass.ds(n * (2 * H * VP) + p * (H * VP), H * VP)].rearrange(
                                      "r (h e) -> r h e", h=H)).then_inc(s["staged"], 1)

            def stage_ctx(stage):
                s = lp[stage]
                cross = stage == "cross"
                vf = (v_ctx if cross else v_last).rearrange("p h b c e -> p (h b c e)")
                to = v_stage if cross else v_stage3
                w = KC * (DV if cross else VP)

                def f(n, p, first):
                    if not first:
                        pool.wait_ge(s["pv"], 4 * n + 2 * p - 2)
                    pool.sem_inc(pool_turn, 1)
                    g.tensor_copy(to[:, 2 * p, :], vf[:, bass.ds((2 * n + p) * w, w)]).then_inc(s["staged"], 1)
                return f

            def negate(s, t, j):
                pool.wait_ge(s["topped"], t + 1)
                g.tensor_tensor(nmax[:, j, 0:1], top[:, j, 0:1], neg_scale[:], ALU.mult).then_inc(s["nm"], 1)

            def take(s, t, j):
                pool.wait_ge(s["masked"], t + 1)
                g.tensor_tensor(e_buf(j), e_buf(j), s2_buf(j), ALU.subtract).then_inc(s["p_ready"], 1)

            def body_self(n, p, first, last):
                if p == 1:
                    if not last:
                        stage_self(n, 0, first)
                elif not first:
                    stage_self(n - 1, 1, type(n) is int and n == 1)

            def body_cross(n, p, first, last):
                stage, s = "cross", lp["cross"]
                t, j = 4 * n + 2 * p, 2 * p
                before = not (first and p == 0)
                if before:
                    take(s, t - 2, (j - 2) % 4)
                if not last:
                    negate(s, t, j)
                    negate(s, t + 1, j + 1)
                if before:
                    take(s, t - 1, (j - 1) % 4)
                if p == 1:
                    stage_ctx(stage)(n, 0, first)
                elif before:
                    stage_ctx(stage)(n - 1, 1, type(n) is int and n == 1)

            def body_last(n, p, first, last):
                stage, s = "last", lp["last"]
                if not last:
                    negate(s, 4 * n + 2 * p, 2 * p)
                    negate(s, 4 * n + 2 * p + 1, 2 * p + 1)
                if p == 1:
                    stage_ctx(stage)(n, 0, first)
                elif not first:
                    stage_ctx(stage)(n - 1, 1, type(n) is int and n == 1)

            def run(N, body):
                for n0 in (0, 1):
                    for p in (0, 1):
                        body(n0, p, n0 == 0, False)
                with pool.Fori(2, N) as n:
                    for p in (0, 1):
                        body(n, p, False, False)
                body(N, 0, False, True)

            last_parts(*SELF_QK)
            last_v_parts("self", 0, NT // 4)
            last_parts(*CROSS_K)
            pool.wait_ge(v_copied, B)
            pool.wait_ge(vals["set"], 2)
            pool.wait_ge(v_pairs_set, 1)
            pool.wait_ge(split["part2"], CROSS_K[1])
            run(NT // 2, body_self)
            run(P // 4, body_cross)
            pool.wait_ge(lp["cross"]["staged"], H * B)
            g.memset(v_last[:, :, :, :, D:VP], 0.0).then_inc(ones_set, 1)
            pool.wait_ge(ones_set, 6)
            g.memset(v_last[:, :, :, :, D:DV], 1.0).then_inc(ones_set, 1)
            last_parts(*LAST_K)
            last_v_parts("last", 0, B)
            pool.wait_ge(vals["set"], 2 + B)
            run(P // 4, body_last)

        @block.scalar
        def _(act):
            s_ = nc.scalar
            act.dma_start(w_kv[:], a["L0_xcond_w_kv"]).then_inc(w_in, 16)
            act.dma_start(w_qkv[:], a["L0_xcond_w_qkv"]).then_inc(w_in, 16)
            load_tables(act, LN_EXP_SET)
            act.wait_ge(x_T, 1)
            s_.activation(chunk(xT, 0), bank[0][:], ACT.Copy).then_inc(xT_set, 1)
            for c in (0, 2):
                act.wait_ge(ctx_T, c + 1)
                s_.activation(chunk(ctxT, c), bank[2 + c][:], ACT.Copy).then_inc(ctxT_set, 1)

            def squares(stage):
                s = ln
                for c in (0, 1):
                    act.wait_ge(s["centred"], LN_AT[stage] + c + 1)
                    s_.activation(sq_of(stage, c), xc_of(stage, c), ACT.Square).then_inc(s["squared"], 1)

            def rstds(stage):
                s = ln
                at = LN_AT[stage]
                eps = LN_OF[stage][3]
                for c in (0, 1):
                    act.wait_ge(s["var_mm"], at + c + 1)
                    s_.activation(sq_of(stage, c), var_bank(stage, c)[:], ACT.Ln, bias=eps).then_inc(s["log_var"], 1)
                for c in (0, 1):
                    act.wait_ge(s["log_var"], at + c + 1)
                    s_.activation(sq_of(stage, c), sq_of(stage, c), ACT.Exp, scale=-0.5).then_inc(s["rstd"], 1)

            def modulate(stage):
                s = ln
                src, dst, chunk0, eps, sc, sh, per = LN_OF[stage]
                if stage == "self":
                    act.wait_ge(mods_set, 2)
                for c in (0, 1) if per == 1 else (0,):
                    act.wait_ge(s["normed"], LN_AT[stage] + c + 1)
                    for i in range(per):
                        b = (chunk0 + c) * per + i
                        n = CH // per
                        s_.activation(dst[:, b * n:(b + 1) * n], xc_of(stage, c)[:, i * n:(i + 1) * n], ACT.Identity,
                                      scale=mods[:, sc, b:b + 1], bias=mods[:, sh, b:b + 1]).then_inc(
                            s["modulated"], 1)

            def first_parts(first, end):
                for n in range(first, end):
                    if n % 2 == 0 and n // 2 in BUFFER_AFTER:
                        act.wait_ge(stacked[BUFFER_AFTER[n // 2]], stacked_by(BUFFER_AFTER[n // 2]))
                    col = UNITS[n][1]
                    act.wait_ge(split["full_mm"], n + 1)
                    s_.activation(part_buf(n, 0), unit_bank(n)[:], ACT.Identity,
                                  bias=cols[:, 1, col:col + 1]).then_inc(split["part0"], 1)

            def first_v_parts(stage, first, end):
                g0 = VALUES[stage][2]
                for i in range(first, end):
                    act.wait_ge(vals["mm"], g0 + i + 1)
                    if i == 0:
                        act.wait_ge(ones_set, 7 if stage == "last" else 5)
                    s_.activation(v_dst(stage, i, 0), v_bank(g0 + i)[:].rearrange("p (t h d) -> p t h d", t=4, h=H),
                                  ACT.Copy).then_inc(vals["part0"], 1)

            def finish_turned(stage):
                vcol = OUT[stage][2]
                for c in range(NX):
                    act.wait_ge(fin["o_T"], NX * FIN_AT[stage] + c + 1)
                    s_.activation(chunk(hT, c), bank[2 * c][:], ACT.Identity,
                                  bias=cols[:, 0, vcol:vcol + 1]).then_inc(fin["oT_set"], 1)

            def finish_projected(stage):
                bcol = OUT[stage][1]
                for c in range(NX):
                    act.wait_ge(fin["y_mm"], NX * FIN_AT[stage] + c + 1)
                    s_.activation(xc_buf(c), bank[2 * c + 1][:], ACT.Identity,
                                  bias=cols[:, 0, bcol:bcol + 1]).then_inc(fin["y_set"], 1)

            def finish(stage):
                finish_turned(stage)
                finish_projected(stage)

            squares("self")
            act.wait_ge(cols_set, 1)
            s_.activation(silu_e[:], cols[:, 0, COND_AT:NVEC], ACT.Exp, scale=-1.0).then_inc(silu_exp, 1)
            rstds("self")
            modulate("self")
            first_parts(*SELF_QK)
            for i in range(B):
                act.wait_ge(vals["mm"], i + 1)
                if i == 0:
                    act.wait_ge(ones_set, 4)
                s_.activation(v_ctx[:, :, i, :, 0:D].rearrange("p h c e -> p c h e"),
                              v_bank(i)[:].rearrange("p (t h d) -> p t h d", t=4, h=H),
                              ACT.Copy).then_inc(v_copied, 1)
            first_v_parts("self", 0, NT // 4)
            first_parts(*CROSS_K)

            s = lp["self"]
            N = NT // 2

            def halves(s, t, j, wait_pv):
                act.wait_ge(s["p_T"], t + 1)
                if wait_pv:
                    act.wait_ge(s["pv"], t - 3)
                s_.activation(pT_part(j, 0), bank[4 + j % 2][:], ACT.Copy, scale=W_UP).then_inc(s["pT_set"], 1)

            def body_self(n, p, first, last):
                t, j = 4 * n + 2 * p, 2 * p
                if not first:
                    for i in (0, 1):
                        halves(s, t - 4 + i, j + i, not (type(n) is int and n == 1))
                if not last:
                    for i in (0, 1):
                        act.wait_ge(s["scanned"], t + i + 1)
                        s_.activation(e_buf(j + i), e_buf(j + i), ACT.Exp, scale=SCALE).then_inc(s["expd"], 1)

            def run(N, body):
                for n0 in (0, 1):
                    for p in (0, 1):
                        body(n0, p, n0 == 0, False)
                with act.Fori(2, N) as n:
                    for p in (0, 1):
                        body(n, p, False, False)
                body(N, 0, False, True)

            run(N, body_self)
            for i in (0, 1):
                halves(s, 4 * N - 2 + i, 2 + i, True)
            finish_turned("self")
            squares("ctx_b")
            finish_projected("self")
            rstds("ctx_b")
            squares("cross")
            rstds("cross")
            modulate("cross")
            modulate("ctx_b")
            first_parts(*CROSS_Q)
            squares("ctx_a")
            rstds("ctx_a")
            modulate("ctx_a")

            s = lp["cross"]
            N = P // 4

            def leave(s, t, j, wait_pv):
                act.wait_ge(s["p_T"], t + 1)
                if wait_pv:
                    act.wait_ge(s["pv"], t - 3)
                s_.activation(pT_buf(j), bank[4 + j % 2][:], ACT.Copy).then_inc(s["pT_set"], 1)

            def rows_out(n):
                act.wait_ge(s["pv"], 4 * n + 4)
                s_.activation(o9[:], bank[O_BANK][0:DV, :], ACT.Copy).then_inc(s["o9_set"], 1)

            def back_out(n):
                act.wait_ge(s["back_T"], n + 1)
                dst = o_raw[:].rearrange("p h t e -> p (h t e)")
                s_.activation(dst[:, bass.ds(n * (4 * DV), 4 * DV)], bank[BACK_BANK][:, 0:4 * DV],
                              ACT.Copy).then_inc(s["o_set"], 1)

            def body_cross(n, p, first, last):
                t, j = 4 * n + 2 * p, 2 * p
                if not (first and p == 0):
                    for i in (0, 1):
                        jj = (j - 2 + i) % 4
                        act.wait_ge(s["marked"], t - 1 + i)
                        s_.activation(s2_buf(jj), s2_buf(jj), ACT.Exp, scale=SCALE,
                                      bias=nmax[:, jj, 0:1]).then_inc(s["masked"], 1)
                if not first:
                    for i in (0, 1):
                        leave(s, t - 4 + i, j + i, not (type(n) is int and n == 1))
                    if not (type(n) is int and n == 1):
                        rows_out(n - 2) if p == 0 else back_out(n - 2)
                if not last:
                    for i in (0, 1):
                        act.wait_ge(s["nm"], t + i + 1)
                        act.wait_ge(s["scanned"], t + i + 1)
                        if not first:
                            act.wait_ge(s["p_T"], t + i - 3)
                        s_.activation(e_buf(j + i), bank[j + i][:], ACT.Exp, scale=SCALE,
                                      bias=nmax[:, j + i, 0:1]).then_inc(s["expd"], 1)

            run(N, body_cross)
            back_out(N - 2)
            for i in (0, 1):
                leave(s, 4 * N - 2 + i, 2 + i, True)
            rows_out(N - 1)
            back_out(N - 1)
            finish("cross")

            squares("mlp")
            first_parts(LAST_K[0], LAST_K[0] + 2)
            rstds("mlp")
            modulate("mlp")
            first_parts(LAST_K[0] + 2, LAST_K[1])
            first_v_parts("last", 0, 2)
            load_tables(act, TANH_SET)
            for u in range(2 * 4):
                c, k = divmod(u, 4)
                bcol = COL["L0_xcond_b_m1"] + k
                act.wait_ge(mlp["a_mm"], u + 1)
                if u >= 2:
                    act.wait_ge(mlp["hidden"], u - 1)
                s_.activation(full_buf(u), bank[2 * (u % 2)][:], ACT.Identity,
                              bias=cols[:, 0, bcol:bcol + 1]).then_inc(mlp["a_set"], 1)
                s_.activation(tanh_buf(u), bank[2 * (u % 2)][:], ACT.Tanh, scale=0.5,
                              bias=half_b1[:, k:k + 1]).then_inc(mlp["tanh_set"], 1)
            for c in range(NX):
                act.wait_ge(mlp["y_part"], 4 * (c + 1))
                bcol = COL["L0_xcond_b_m2"]
                s_.activation(xc_buf(c), bank[4 + c][:], ACT.Identity, scale=0.5,
                              bias=cols[:, 0, bcol:bcol + 1]).then_inc(mlp["y_set"], 1)

            load_tables(act, LN_EXP_SET)
            squares("last")
            first_v_parts("last", 2, B)
            rstds("last")
            modulate("last")
            first_parts(*LAST_Q)
            s = lp["last"]

            def body_last(n, p, first, last):
                t, j = 4 * n + 2 * p, 2 * p
                if not first:
                    for i in (0, 1):
                        halves(s, t - 4 + i, j + i, not (type(n) is int and n == 1))
                if not last:
                    for i in (0, 1):
                        act.wait_ge(s["nm"], t + i + 1)
                        if not first:
                            act.wait_ge(s["p_T"], t + i - 3)
                        s_.activation(e_buf(j + i), bank[j + i][:], ACT.Exp, scale=SCALE,
                                      bias=nmax[:, j + i, 0:1]).then_inc(s["expd"], 1)

            run(N, body_last)
            for i in (0, 1):
                halves(s, 4 * N - 2 + i, 2 + i, True)
            finish("last")
            act.wait_ge(out_T, 1)
            s_.activation(tok[:, 0:4, :].rearrange("p t f -> p (t f)"), bank[0][:], ACT.Copy).then_inc(out_set[0], 1)

        @block.vector
        def _(dve):
            v = nc.vector
            v.memset(q_stack[:].bitcast(F32), 0.0).then_inc(zeros_set, 1)
            dve.wait_ge(x_T, 2)
            v.tensor_copy(chunk(xT, 1), bank[1][:]).then_inc(xT_set, 1)
            for c in (1, 3):
                dve.wait_ge(ctx_T, c + 1)
                v.tensor_copy(chunk(ctxT, c), bank[2 + c][:]).then_inc(ctxT_set, 1)

            def centre(stage):
                s = ln
                at = LN_AT[stage]
                src, dst, chunk0, eps, sc, sh, per = LN_OF[stage]
                for c in (0, 1):
                    dve.wait_ge(s["mean_mm"], at + c + 1)
                    if stage not in ("self", "ctx_b"):
                        dve.wait_ge(s["modulated"], MODULATED_AT[stage])
                        dve.wait_ge(s["modulated_v"], MODULATED_V_BEFORE[stage])
                    v.tensor_tensor(xc_of(stage, c), chunk(src, chunk0 + c), mean_bank(stage, c)[:],
                                    ALU.subtract).then_inc(s["centred"], 1)

            def scale(stage):
                s = ln
                for c in (0, 1):
                    dve.wait_ge(s["rstd"], LN_AT[stage] + c + 1)
                    v.tensor_tensor(xc_of(stage, c), xc_of(stage, c), sq_of(stage, c), ALU.mult).then_inc(s["normed"], 1)

            def modulate(stage):
                src, dst, chunk0, eps, sc, sh, per = LN_OF[stage]
                dve.wait_ge(ln["normed"], LN_AT[stage] + 2)
                for i in range(2):
                    b = 2 + i
                    last = v.tensor_scalar(dst[:, b * L:(b + 1) * L], xc_buf(1)[:, i * L:(i + 1) * L],
                                           mods[:, sc, b:b + 1], mods[:, sh, b:b + 1], ALU.mult, ALU.add)
                last.then_inc(ln["modulated_v"], 1)

            def middle_parts(first, end):
                for n0 in range(first, end, 2):
                    for n in (n0, n0 + 1):
                        dve.wait_ge(split["part0"], n + 1)
                        if n >= 2:
                            dve.wait_ge(split["part2"], n - 1)
                        col = UNITS[n][1]
                        v.scalar_tensor_tensor(rest_buf(n), unit_bank(n)[:], cols[:, 1, col:col + 1], part_buf(n, 0),
                                               ALU.add, ALU.subtract).then_inc(split["rest"], 1)
                    for n in (n0, n0 + 1):
                        dve.wait_ge(split["rest"], n + 1)
                        v.tensor_copy(part_buf(n, 1), rest_buf(n)).then_inc(split["part1"], 1)
                    if n0 in (CROSS_Q[0], LAST_Q[0]):
                        dve.wait_ge(split["part2"], n0)
                        for n in (n0, n0 + 1):
                            dve.wait_ge(split["part1"], n + 1)
                            v.tensor_tensor(part_buf(n, 2), rest_buf(n), part_buf(n, 1), ALU.subtract).then_inc(
                                split["part2"], 1)

            def middle_v_parts(stage, first, end):
                g0 = VALUES[stage][2]
                for i in range(first, end):
                    rest = v_rest_buf(stage, i).rearrange("p (t h d) -> p t h d", t=4, h=H)
                    m = v_number(g0, i)
                    dve.wait_ge(vals["part0"], m + 1)
                    if stage == "self" and i == 0:
                        dve.wait_ge(ones_set, 5)
                    if i >= 2:
                        dve.wait_ge(vals["set"], m - 1)
                    v.tensor_tensor(rest, v_bank(g0 + i)[:].rearrange("p (t h d) -> p t h d", t=4, h=H),
                                    v_dst(stage, i, 0), ALU.subtract).then_inc(v_read, 1)
                    dve.wait_ge(v_read, m + 1)
                    v.tensor_copy(v_dst(stage, i, 1), rest).then_inc(vals["rest"], 1)

            def finish_normed(stage):
                dve.wait_ge(lp[stage]["o_set"], NT if stage == "self" else P // 4)
                v.reciprocal(rden[:], o_raw[:, :, :, D]).then_inc(fin["recip"], 1)
                dve.wait_ge(fin["recip"], FIN_AT[stage] + 1)
                for c in range(NX):
                    t = slice(4 * c, 4 * c + 4)
                    v.tensor_tensor(tok[:, t, :].rearrange("p t (h d) -> p h t d", h=H), o_raw[:, :, t, 0:D],
                                    rden[:, :, t].unsqueeze(3).broadcast_to([P, H, 4, D]),
                                    ALU.mult).then_inc(fin["o_norm"], 1)

            def finish_added(stage):
                g = OUT[stage][3]
                for c in range(NX):
                    dve.wait_ge(fin["y_set"], NX * FIN_AT[stage] + c + 1)
                    if g is None:
                        v.tensor_tensor(chunk(xT, c), chunk(xT, c), xc_buf(c), ALU.add).then_inc(fin["x_new"], 1)
                    else:
                        for i in range(2):
                            b = 2 * c + i
                            xb = xT[:, b * L:(b + 1) * L]
                            last = v.scalar_tensor_tensor(xb, xc_buf(c)[:, i * L:(i + 1) * L], mods[:, g, b:b + 1], xb,
                                                          ALU.mult, ALU.add)
                        last.then_inc(fin["x_new"], 1)

            def finish(stage):
                finish_normed(stage)
                finish_added(stage)

            centre("self")
            dve.wait_ge(vec_in, 16 * (len(VECTORS) + 1))
            v.tensor_copy(vecs_p[:].rearrange("r (d h) -> r d h", h=H),
                          vecs[:].rearrange("r (h d) -> r d h", h=H)).then_inc(vecs_set, 1)
            dve.wait_ge(cols_T, 1)
            v.tensor_copy(cols[:].rearrange("p a n -> p (a n)"), bank[7][:, 0:2 * NVEC]).then_inc(cols_set, 1)
            dve.wait_ge(cols_set, 1)
            v.tensor_scalar(half_b1[:], cols[:, 0, COL["L0_xcond_b_m1"]:COL["L0_xcond_b_m1"] + 4], 0.5, None,
                            ALU.mult).then_inc(cols_set, 1)
            dve.wait_ge(silu_exp, 1)
            v.tensor_scalar(silu_e[:], silu_e[:], 1.0, None, ALU.add).then_inc(cond_step, 1)
            dve.wait_ge(cond_step, 1)
            v.reciprocal(silu_e[:], silu_e[:]).then_inc(cond_step, 1)
            dve.wait_ge(cond_step, 2)
            v.tensor_tensor(silu_c[:], cols[:, 0, COND_AT:NVEC], silu_e[:], ALU.mult).then_inc(silu_set, 1)
            scale("self")
            dve.wait_ge(mods_mm, 1)
            v.tensor_tensor(mods[:], bank[6][:, 0:NMOD * B].rearrange("p (m b) -> p m b", b=B),
                            cols[:, 0, 0:NMOD].unsqueeze(2).broadcast_to([P, NMOD, B]), ALU.add).then_inc(mods_set, 1)
            dve.wait_ge(mods_set, 1)
            scales = mods[:, 1:13, :].rearrange("p (m r) b -> p m r b", r=3)[:, 0:3, 0, :]
            v.tensor_scalar(scales, scales, 1.0, None, ALU.add).then_inc(cond_step, 1)
            scales = mods[:, 9:13, :].rearrange("p (m r) b -> p m r b", r=2)[:, :, 0, :]
            v.tensor_scalar(scales, scales, 1.0, None, ALU.add).then_inc(cond_step, 1)
            dve.wait_ge(cond_step, 4)
            dve.sem_inc(mods_set, 1)
            modulate("self")
            middle_parts(*SELF_QK)
            middle_v_parts("self", 0, NT // 4)
            middle_parts(*CROSS_K)

            s = lp["self"]

            def maxima_self(t, j0, first):
                for i in (0, 1):
                    j = j0 + i
                    dve.wait_ge(s["scores"], t + i + 1)
                    v.tensor_reduce(nmax[:, j, :], bank[j][:].rearrange("p (h k) -> p h k", h=8), AX_X,
                                    ALU.max).then_inc(s["topped"], 1)
                for i in (0, 1):
                    j = j0 + i
                    dve.wait_ge(s["topped"], t + i + 1)
                    if not first:
                        dve.wait_ge(s["p_T"], t + i - 3)
                    v.tensor_tensor(e_buf(j).rearrange("p (h k) -> p h k", h=8),
                                    bank[j][:].rearrange("p (h k) -> p h k", h=8),
                                    nmax[:, j, :].unsqueeze(2).broadcast_to([P, 8, WIN]),
                                    ALU.subtract).then_inc(s["scanned"], 1)

            def attend(s, N, maxima, sums):
                def body(n, p, first, last):
                    t, j = 4 * n + 2 * p, 2 * p
                    if not first:
                        for i in (0, 1):
                            rests(s, t - 4 + i, j + i)
                    if p == 1 and not first:
                        sums(n - 1, 0)
                    if p == 0 and not first and not (type(n) is int and n == 1):
                        sums(n - 2, 1)
                    if p == 0:
                        maxima(t + 2, 2, first)
                    elif not last:
                        maxima(t + 2, 0, False)

                maxima(0, 0, True)
                for n0 in (0, 1):
                    for p in (0, 1):
                        body(n0, p, n0 == 0, False)
                with dve.Fori(2, N - 1) as n:
                    for p in (0, 1):
                        body(n, p, False, False)
                for p in (0, 1):
                    body(N - 1, p, False, True)
                for i in (0, 1):
                    rests(s, 4 * N - 4 + i, i)
                sums(N - 2, 1)
                for i in (0, 1):
                    rests(s, 4 * N - 2 + i, 2 + i)
                sums(N - 1, 0)
                sums(N - 1, 1)

            def run(N, body):
                for n0 in (0, 1):
                    for p in (0, 1):
                        body(n0, p, n0 == 0, False)
                with dve.Fori(2, N) as n:
                    for p in (0, 1):
                        body(n, p, False, False)

            def rests(s, t, j):
                dve.wait_ge(s["pT_set"], t + 1)
                v.scalar_tensor_tensor(pT_part(j, 1), bank[4 + j % 2][:], W_UP, pT_part(j, 0), ALU.mult,
                                       ALU.subtract).then_inc(s["rest_set"], 1)

            def sums_self(n, p):
                dve.wait_ge(s["pv"], 4 * n + 2 * p + 2)
                v.tensor_reduce(o_raw[:, :, bass.ds(n * 2 + p, 1), :].rearrange("p h t e -> p (h t) e"),
                                bank[O_BANK + p][:, 0:H * VP].rearrange("p (h s e) -> p h e s", h=H, s=3), AX_X,
                                ALU.add).then_inc(s["o_set"], 1)

            def sums_last(n, p):
                if p == 0:
                    return
                dve.wait_ge(s["pv"], 4 * n + 4)
                dst = o_raw[:].rearrange("p h t e -> p (h t e)")[:, bass.ds(n * (4 * DV), 4 * DV)]
                v.tensor_reduce(dst.rearrange("p (t e) -> p t e", t=4),
                                bank[O_BANK][:, 0:4 * VP].rearrange("p (t s e) -> p t e s", t=4, s=3), AX_X,
                                ALU.add).then_inc(s["o_set"], 1)

            attend(s, NT // 2, maxima_self, sums_self)
            finish_normed("self")
            centre("ctx_b")
            finish_added("self")
            scale("ctx_b")
            centre("cross")
            scale("cross")
            modulate("cross")
            middle_parts(*CROSS_Q)
            centre("ctx_a")
            scale("ctx_a")

            s = lp["cross"]

            def body_cross(n, p, first, last):
                t, j0 = 4 * n + 2 * p, 2 * p
                for i in (0, 1):
                    j = j0 + i
                    dve.wait_ge(s["scores"], t + i + 1)
                    dve.sem_inc(turn, 1)
                    v.max(top[:, j, 0:8], bank[j][:]).then_inc(s["topped"], 1)
                for i in (0, 1):
                    j = j0 + i
                    dve.wait_ge(s["topped"], t + i + 1)
                    dve.sem_inc(turn, 1)
                    v.match_replace(s1_buf(j), top[:, j, 0:8], bank[j][:], TAKEN).then_inc(s["scanned"], 1)
                for i in (0, 1):
                    j = j0 + i
                    dve.wait_ge(s["scanned"], t + i + 1)
                    dve.sem_inc(turn, 1)
                    v.max(top[:, j, 8:16], s1_buf(j)).then_inc(chain, 1)
                for i in (0, 1):
                    j = j0 + i
                    dve.wait_ge(chain, t + i + 1)
                    if not first:
                        dve.wait_ge(s["p_ready"], t + i - 3)
                    dve.sem_inc(turn, 1)
                    v.match_replace(s2_buf(j), top[:, j, 8:16], s1_buf(j), TAKEN).then_inc(s["marked"], 1)

            run(P // 4, body_cross)
            finish("cross")

            centre("mlp")
            middle_parts(LAST_K[0], LAST_K[0] + 2)
            scale("mlp")
            modulate("mlp")
            middle_parts(LAST_K[0] + 2, LAST_K[1])
            middle_v_parts("last", 0, 2)
            for u in range(2 * 4):
                c, k = divmod(u, 4)
                bcol = COL["L0_xcond_b_m1"] + 4 + k
                dve.wait_ge(mlp["tanh_set"], u + 1)
                v.scalar_tensor_tensor(full_buf(u), tanh_buf(u), 1.0, full_buf(u), ALU.add,
                                       ALU.mult).then_inc(mlp["gated"], 1)
                dve.wait_ge(mlp["gated"], u + 1)
                dve.wait_ge(mlp["b_mm"], u + 1)
                if u >= 2:
                    dve.wait_ge(mlp["y_part"], u - 1)
                v.scalar_tensor_tensor(sq_buf(u), bank[2 * (u % 2) + 1][:], cols[:, 0, bcol:bcol + 1], full_buf(u),
                                       ALU.add, ALU.mult).then_inc(mlp["hidden"], 1)
            for c in range(NX):
                dve.wait_ge(mlp["y_set"], c + 1)
                for i in range(2):
                    b = 2 * c + i
                    xb = xT[:, b * L:(b + 1) * L]
                    last = v.scalar_tensor_tensor(xb, xc_buf(c)[:, i * L:(i + 1) * L], mods[:, G_MLP, b:b + 1], xb,
                                                  ALU.mult, ALU.add)
                last.then_inc(mlp["x_new"], 1)

            centre("last")
            middle_v_parts("last", 2, B)
            scale("last")
            modulate("last")
            middle_parts(*LAST_Q)
            s = lp["last"]

            def maxima_last(t, j0, first):
                for i in (0, 1):
                    dve.wait_ge(s["scores"], t + i + 1)
                    if not first:
                        dve.wait_ge(s["expd"], t + i - 3)
                    v.tensor_reduce(top[:, j0 + i, 0:1], bank[j0 + i][:], AX_X, ALU.max).then_inc(s["topped"], 1)

            attend(s, P // 4, maxima_last, sums_last)
            finish("last")
            dve.wait_ge(out_T, 2)
            v.tensor_copy(tok[:, 4:8, :].rearrange("p t f -> p (t f)"), bank[1][:]).then_inc(out_set[1], 1)

        @block.tensor
        def _(pe):
            t_ = nc.tensor
            mm = t_.matmul
            pe.wait_ge(ident_set, 2)
            pe.wait_ge(x_in, 48)
            for t in range(NT):
                last = t_.transpose(bank[t // 4][:, (t % 4) * P:(t % 4 + 1) * P], tok[:, t, :], ident[:])
                if t % 4 == 3:
                    last.then_inc(x_T, 1)
            pe.wait_ge(ctx_in, 16)
            for t in range(NCT):
                last = t_.transpose(bank[2 + t // 4][:, (t % 4) * P:(t % 4 + 1) * P], ctx_tok[:, t, :], ident[:])
                if t % 4 == 3:
                    last.then_inc(ctx_T, 1)

            def means(stage):
                s = ln
                src, dst, chunk0, eps, sc, sh, per = LN_OF[stage]
                if stage in x_before:
                    pe.wait_ge(*x_before[stage])
                for c in (0, 1):
                    mm(mean_bank(stage, c)[:], mean_w[:], chunk(src, chunk0 + c), start=True,
                       stop=True).then_inc(s["mean_mm"], 1)

            def variances(stage):
                s = ln
                for c in (0, 1):
                    pe.wait_ge(s["squared"], LN_AT[stage] + c + 1)
                    mm(var_bank(stage, c)[:], mean_w[:], sq_of(stage, c), start=True, stop=True).then_inc(s["var_mm"], 1)

            def project(first, end):
                for n in range(first, end):
                    w, _, src, c = UNITS[n]
                    if src is hT:
                        stage = "self" if n < CROSS_Q[0] else "cross" if n < LAST_K[0] else "last"
                        if c == 0:
                            pe.wait_ge(ln["modulated"], MODULATED_AT[stage] + 2)
                        else:
                            pe.wait_ge(ln["modulated_v"], MODULATED_V_BEFORE[stage] + 1)
                    if n >= 2:
                        pe.wait_ge(split["rest"], n - 1)
                    mm(unit_bank(n)[:], w, chunk(src, c), start=True, stop=True).then_inc(split["full_mm"], 1)

            def values(stage, first, end):
                w, src, g0, groups = VALUES[stage]
                for i in range(first, end):
                    if g0 + i >= B + 2:
                        pe.wait_ge(v_read, g0 + i - B - 1)
                    elif g0 + i >= 2:
                        pe.wait_ge(v_copied, g0 + i - 1)
                    for k in range(4):
                        t = 4 * i + k
                        if stage != "self":
                            last = mm(v_bank(g0 + i)[:, k * C:(k + 1) * C], src[:, t * P:(t + 1) * P], w, start=True,
                                      stop=True)
                            continue
                        by_parity = w.rearrange("p (i r d) -> p r i d", r=2, d=D)
                        for win in (0, 1):
                            at = t * P + win * WIN
                            for par in (0, 1):
                                last = mm(v_bank(g0 + i)[64 * par:64 * par + 64,
                                                         k * C + win * WIN:k * C + (win + 1) * WIN],
                                          src[:, at:at + WIN], by_parity[:, par], start=True, stop=True)
                    last.then_inc(vals["mm"], 1)

            def left(s, n, j, more):
                name = "pT_set" if s is lp["cross"] else "rest_set"
                pe.wait_ge(s[name], 4 * n + j + (1 if more else -1))

            def transposes(s, n, j, ready, first):
                pe.wait_ge(s[ready], 4 * n + j + 1)
                if not (first and j < 2):
                    left(s, n, j, 0)
                for i in range(4):
                    last = t_.transpose(bank[4 + j % 2][:, i * P:(i + 1) * P], e_buf(j)[:, i * P:(i + 1) * P], ident[:])
                last.then_inc(s["p_T"], 1)

            def finish(stage):
                s = fin
                w, bcol, vcol, g = OUT[stage]
                for c in range(NX):
                    pe.wait_ge(s["o_norm"], NX * FIN_AT[stage] + c + 1)
                    for i in range(4):
                        last = t_.transpose(bank[2 * c][:, i * P:(i + 1) * P], tok[:, 4 * c + i, :], ident[:])
                    last.then_inc(s["o_T"], 1)
                for c in range(NX):
                    pe.wait_ge(s["oT_set"], NX * FIN_AT[stage] + c + 1)
                    mm(bank[2 * c + 1][:], w, chunk(hT, c), start=True, stop=True).then_inc(s["y_mm"], 1)

            def wait_stacked(*pairs):
                for pair in pairs:
                    pe.wait_ge(stacked[pair], stacked_by(pair))

            pe.wait_ge(ones_set, 2)
            pe.wait_ge(ctxT_set, 4)
            means("self")
            pe.wait_ge(vec_in, 16 * (len(VECTORS) + 1))
            pe.wait_ge(vecs_set, 1)
            t_.transpose(bank[7][:, 0:NVEC], vecs[:], ident[0:NVEC, 0:NVEC])
            t_.transpose(bank[7][:, NVEC:2 * NVEC], vecs_p[:],
                         ident[0:NVEC, 0:NVEC]).then_inc(cols_T, 1)
            variances("self")
            pe.wait_ge(ada_in, 48)
            pe.wait_ge(silu_set, 1)
            for m in range(NMOD):
                w = w_ada[:, m * C:(m + 1) * C] if m < 9 else w_ss[:, (m - 9) * C:(m - 8) * C]
                last = mm(bank[6][:, m * B:(m + 1) * B], w, silu_c[:], start=True, stop=True)
            last.then_inc(mods_mm, 1)
            pe.wait_ge(w_qk_set, 3)
            project(*SELF_QK)
            pe.wait_ge(mods_set, 1)
            values("cross", 0, B)
            values("self", 0, NT // 4)
            project(*CROSS_K)
            pe.wait_ge(split["part2"], CROSS_K[1])
            pe.wait_ge(vals["set"], 2)
            pe.wait_ge(v_copied, B)
            pe.wait_ge(zeros_set, 1)
            wait_stacked(0, 1)

            s = lp["self"]

            def scores_self(n, j, first):
                t = 4 * n + j
                if not first:
                    pe.wait_ge(s["scanned"], t - 3)
                for i in range(8):
                    tile, h = j // 2, 8 * (j % 2) + i
                    last = mm(bank[j][:, i * WIN:(i + 1) * WIN],
                              q_stack[0:KW, bass.ds(n * (2 * P) + (h * NTOK + tile * P), P)],
                              k_windows[0:KW, bass.ds(n * (2 * WIN) + (h * NT + tile) * WIN, WIN)],
                              start=True, stop=True)
                last.then_inc(s["scores"], 1)

            def pv_self(n, p, first):
                for half in (0, 1):
                    j = 2 * p + half
                    left(s, n, j, 1)
                    if half == 0:
                        pe.wait_ge(s["staged"], 2 * (2 * n + p + 1))
                        if not first:
                            pe.wait_ge(s["o_set"], 2 * n + p - 1)
                    for i in range(4):
                        g = 4 * half + i
                        for win in (0, 1):
                            for part in (0, 1):
                                at = i * P + win * WIN
                                last = mm(bank[O_BANK + p][64 * win:64 * win + 64, 2 * g * VP:2 * (g + 1) * VP],
                                          pT_part(j, part)[:, at:at + WIN],
                                          v_pairs[:, p, win * (H // 2) + g].rearrange("p r e -> p (r e)"),
                                          start=(part == 0), stop=(part == 1))
                    last.then_inc(s["pv"], 1)

            def attend(s, N, scores, pv, ready, back=None):
                def body(n, p, first, last):
                    for i in (0, 1):
                        if p == 0:
                            scores(n, 2 + i, first)
                        elif not last:
                            scores(n + 1, i, False)
                    if back and p == 1 and not first and not (type(n) is int and n == 1):
                        back(n - 2)
                    for i in (0, 1):
                        if p == 1:
                            transposes(s, n, i, ready, first)
                        elif not first:
                            transposes(s, n - 1, 2 + i, ready, type(n) is int and n == 1)
                    if not first:
                        pv(n - 1, p, type(n) is int and n == 1)

                scores(0, 0, True)
                scores(0, 1, True)
                for n0 in (0, 1):
                    for p in (0, 1):
                        body(n0, p, n0 == 0, False)
                with pe.Fori(2, N - 1) as n:
                    for p in (0, 1):
                        body(n, p, False, False)
                for p in (0, 1):
                    body(N - 1, p, False, True)
                if back:
                    back(N - 2)
                for i in (0, 1):
                    transposes(s, N - 1, 2 + i, ready, False)
                for p in (0, 1):
                    pv(N - 1, p, False)
                if back:
                    back(N - 1)

            attend(s, NT // 2, scores_self, pv_self, "expd")
            pe.wait_ge(w_late_in, 16 * N_LATE)
            pe.wait_ge(w_qk_set, 6)
            means("ctx_b")
            finish("self")
            variances("ctx_b")
            means("cross")
            variances("cross")
            project(*CROSS_Q)
            means("ctx_a")
            variances("ctx_a")
            pe.wait_ge(ln["modulated"], MODULATED_AT["ctx_a"] + 2)
            pe.wait_ge(split["part2"], CROSS_Q[1])
            wait_stacked(2, 3, 4)

            def scores_ctx(s, frees):
                def f(n, j, first):
                    t = 4 * n + j
                    if not first:
                        for name in frees:
                            pe.wait_ge(s[name], t - 3)
                    g = 2 * n + j // 2
                    mm(bank[j][:], q_stack[0:KS, bass.ds(g * L + (j % 2) * P, P)], k_stack[0:KS, bass.ds(g * LC, LC)],
                       start=True, stop=True).then_inc(s["scores"], 1)
                return f

            def pv_cross(n, p, first):
                s = lp["cross"]
                left(s, n, 2 * p + 1, 1)
                pe.wait_ge(s["staged"], 2 * n + p + 1)
                if p == 0 and not first:
                    pe.wait_ge(s["o9_set"], n)
                for c in range(KC):
                    last = mm(bank[O_BANK][0:DV, 2 * p * P:2 * (p + 1) * P], v_stage[:, 2 * p, c * DV:(c + 1) * DV],
                              pT_pair[:, 2 * p:2 * p + 2, c * P:(c + 1) * P], start=(c == 0), stop=(c == KC - 1))
                last.then_inc(s["pv"], 2)

            def back_cross(n):
                s = lp["cross"]
                pe.wait_ge(s["o9_set"], n + 1)
                pe.sem_inc(pe_turn, 1)
                for j in range(4):
                    last = t_.transpose(bank[BACK_BANK][:, j * DV:(j + 1) * DV], o9[:, j * P:(j + 1) * P],
                                        ident[0:DV, 0:DV])
                last.then_inc(s["back_T"], 1)

            def pv_last(n, p, first):
                s = lp["last"]
                for j in (2 * p, 2 * p + 1):
                    left(s, n, j, 1)
                    pe.wait_ge(s["staged"], 2 * n + p + 1)
                    if j == 0 and not first:
                        pe.wait_ge(s["o_set"], n)
                    for c in range(KC):
                        for part in (0, 1):
                            last = mm(bank[O_BANK][:, j * VP:(j + 1) * VP], pT_part(j, part)[:, c * P:(c + 1) * P],
                                      v_stage3[:, 2 * p, c * VP:(c + 1) * VP], start=(c == 0 and part == 0),
                                      stop=(c == KC - 1 and part == 1))
                    last.then_inc(s["pv"], 1)

            s = lp["cross"]
            attend(s, P // 4, scores_ctx(s, ("expd",)), pv_cross, "p_ready", back_cross)
            pe.wait_ge(s["o_set"], P // 4)
            finish("cross")

            means("mlp")
            project(LAST_K[0], LAST_K[0] + 2)
            variances("mlp")
            project(LAST_K[0] + 2, LAST_K[1])
            values("last", 0, 2)
            pe.wait_ge(ln["modulated"], MODULATED_AT["mlp"] + 2)

            def down(u):
                c, k = divmod(u, 4)
                if u == 0:
                    pe.wait_ge(split["rest"], LAST_K[1])
                pe.wait_ge(mlp["hidden"], u + 1)
                last = mm(bank[4 + c][:], w_m2[:, k, :], sq_buf(u), start=(k == 0), stop=(k == 3))
                last.then_inc(mlp["y_part"], 1)

            for u in range(2 * 4):
                c, k = divmod(u, 4)
                if u == 4:
                    pe.wait_ge(ln["modulated_v"], MODULATED_V_BEFORE["mlp"] + 1)
                if u >= 2:
                    pe.wait_ge(mlp["tanh_set"], u - 1)
                mm(bank[2 * (u % 2)][:], w_m1[:, k * P:(k + 1) * P], chunk(hT, c), start=True,
                   stop=True).then_inc(mlp["a_mm"], 1)
                if u >= 2:
                    down(u - 2)
                mm(bank[2 * (u % 2) + 1][:], w_m1[:, HID + k * P:HID + (k + 1) * P], chunk(hT, c), start=True,
                   stop=True).then_inc(mlp["b_mm"], 1)
            down(6)
            down(7)

            means("last")
            values("last", 2, B)
            variances("last")
            project(*LAST_Q)
            pe.wait_ge(vals["set"], 2 + B)
            wait_stacked(5, 6, 7)
            s = lp["last"]
            attend(s, P // 4, scores_ctx(s, ("expd",)), pv_last, "expd")
            finish("last")
            for c in range(NX):
                pe.wait_ge(fin["x_new"], 2 * NX + c + 1)
                for i in range(4):
                    t = 4 * c + i
                    last = t_.transpose(bank[c][:, i * P:(i + 1) * P], xT[:, t * P:(t + 1) * P], ident[:])
                last.then_inc(out_T, 1)


_OUT_SHAPE = (B, L, C)


def kernel(**inputs):
    import numpy as _np
    import concourse.bacc as _bacc
    from concourse.bass_utils import run_bass_kernel_spmd as _run

    nc = _bacc.Bacc("TRN2", target_bir_lowering=False, num_devices=1)
    arrays, args = {}, {}
    for name, value in inputs.items():
        value = _np.ascontiguousarray(value)
        arrays[f"in_{name}"] = value
        args[name] = nc.dram_tensor(f"in_{name}", value.shape, mybir.dt.from_np(value.dtype), kind="ExternalInput").ap()
    out = nc.dram_tensor("out", _OUT_SHAPE, F32, kind="ExternalOutput").ap()
    pixart_kernel(nc, args, out)
    r = _run(nc, [arrays], core_ids=[0])
    return r.results[0]["out"]
```
